# Optimizing a Trainium2 kernel written in Bass

```python
import numpy as np
import jax
import jax.numpy as jnp

def _softmax(x, axis=-1):
    return jax.nn.softmax(x, axis=axis)
def _gelu(x):
    return jax.nn.gelu(x, approximate=True)
def _silu(x):
    return jax.nn.silu(x)
def _sigmoid(x):
    return jax.nn.sigmoid(x)
def _layernorm(x, axis=-1, eps=1e-5):
    m = jnp.mean(x, axis=axis, keepdims=True)
    v = jnp.var(x, axis=axis, keepdims=True)
    return (x - m) / jnp.sqrt(v + eps)
def _scatter_add(tgt, idx, src, axis=0):
    return tgt.at[idx].add(src)
def _segment_sum(src, seg, n):
    return jax.ops.segment_sum(src, seg, n)

kernel_name = 'mk_conv_preact_d2_conv_nchw256_75f7cd'

def setup_inputs(seed: int = 0):
    np.random.seed(seed)
    _w = jnp.asarray
    def _rec_inputs():
        import jax
        import jax.numpy as jnp
        _gk = jax.random.key(seed)
        x = -0.0002928 + 1 * jax.random.normal(jax.random.fold_in(_gk, 1), (4, 256, 64, 64), jnp.float32)
        return x
    x = _rec_inputs()
    def _L0_conv_setup():
        import jax, jax.numpy as jnp
        import numpy as np
        C = 256
        CK = C // 8
        key = jax.random.key(seed)
        ks = jax.random.split(key, 7)
        sc = 0.05
        x = jax.random.normal(ks[0], (4, C, 64, 64), dtype=jnp.float32)
        Wq = jax.random.normal(ks[1], (CK, C), dtype=jnp.float32) * sc
        bq = jax.random.normal(ks[2], (CK,), dtype=jnp.float32) * sc
        Wk = jax.random.normal(ks[3], (CK, C), dtype=jnp.float32) * sc
        bk = jax.random.normal(ks[4], (CK,), dtype=jnp.float32) * sc
        Wv = jax.random.normal(ks[5], (C, C), dtype=jnp.float32) * sc
        bv = jax.random.normal(ks[6], (C,), dtype=jnp.float32) * sc
        gamma = jnp.array([0.5], dtype=jnp.float32)
        return {'x': x, 'Wq': Wq, 'bq': bq, 'Wk': Wk, 'bk': bk, 'Wv': Wv, 'bv': bv, 'gamma': gamma}
    _L0_conv_all = _L0_conv_setup()
    _L0_conv_in = {k: v for k, v in _L0_conv_all.items() if k in ('Wq', 'bq', 'Wk', 'bk', 'Wv', 'bv', 'gamma', )}
    del _L0_conv_all

    def _L1_conv_setup():
        import jax, jax.numpy as jnp
        import numpy as np
        C_MID = 32
        _ROWS = np.concatenate([np.arange(C_MID - i) + i for i in range(C_MID)])
        _COLS = np.concatenate([np.arange(C_MID - i) for i in range(C_MID)])

        def _bn_relu(y, g, b, m, v, eps=1e-05):
            inv = g / jnp.sqrt(v + eps)
            return jax.nn.relu(y * inv[:, None, None] + (b - m * inv)[:, None, None])
        key = jax.random.key(seed)
        ks = jax.random.split(key, 14)
        B, Cin, H, W = (16, 256, 64, 64)
        mid, T, Cout = (C_MID, C_MID * (C_MID + 1) // 2, 256)
        return {'x': jax.random.normal(ks[0], (B, Cin, H, W), jnp.float32), 'w1': jax.random.normal(ks[1], (mid, Cin), jnp.float32) * 0.05, 'b1': jax.random.normal(ks[2], (mid,), jnp.float32) * 0.05, 'g1': jax.random.uniform(ks[3], (mid,), jnp.float32, 0.5, 1.5), 'be1': jax.random.normal(ks[4], (mid,), jnp.float32) * 0.1, 'm1': jax.random.normal(ks[5], (mid,), jnp.float32) * 0.1, 'v1': jax.random.uniform(ks[6], (mid,), jnp.float32, 0.5, 1.5), 'w2': jax.random.normal(ks[7], (Cout, T), jnp.float32) * 0.05, 'b2': jax.random.normal(ks[8], (Cout,), jnp.float32) * 0.05, 'g2': jax.random.uniform(ks[9], (Cout,), jnp.float32, 0.5, 1.5), 'be2': jax.random.normal(ks[10], (Cout,), jnp.float32) * 0.1, 'm2': jax.random.normal(ks[11], (Cout,), jnp.float32) * 0.1, 'v2': jax.random.uniform(ks[12], (Cout,), jnp.float32, 0.5, 1.5)}
    _L1_conv_all = _L1_conv_setup()
    _L1_conv_in = {k: v for k, v in _L1_conv_all.items() if k in ('w1', 'b1', 'g1', 'be1', 'm1', 'v1', 'w2', 'b2', 'g2', 'be2', 'm2', 'v2', )}
    del _L1_conv_all

    return {
        "x": x,
        "L0_conv_Wq": _L0_conv_in["Wq"],
        "L0_conv_bq": _L0_conv_in["bq"],
        "L0_conv_Wk": _L0_conv_in["Wk"],
        "L0_conv_bk": _L0_conv_in["bk"],
        "L0_conv_Wv": _L0_conv_in["Wv"],
        "L0_conv_bv": _L0_conv_in["bv"],
        "L0_conv_gamma": _L0_conv_in["gamma"],
        "L1_conv_w1": _L1_conv_in["w1"],
        "L1_conv_b1": _L1_conv_in["b1"],
        "L1_conv_g1": _L1_conv_in["g1"],
        "L1_conv_be1": _L1_conv_in["be1"],
        "L1_conv_m1": _L1_conv_in["m1"],
        "L1_conv_v1": _L1_conv_in["v1"],
        "L1_conv_w2": _L1_conv_in["w2"],
        "L1_conv_b2": _L1_conv_in["b2"],
        "L1_conv_g2": _L1_conv_in["g2"],
        "L1_conv_be2": _L1_conv_in["be2"],
        "L1_conv_m2": _L1_conv_in["m2"],
        "L1_conv_v2": _L1_conv_in["v2"],
    }

def reference(x, L0_conv_Wq, L0_conv_bq, L0_conv_Wk, L0_conv_bk, L0_conv_Wv, L0_conv_bv, L0_conv_gamma, L1_conv_w1, L1_conv_b1, L1_conv_g1, L1_conv_be1, L1_conv_m1, L1_conv_v1, L1_conv_w2, L1_conv_b2, L1_conv_g2, L1_conv_be2, L1_conv_m2, L1_conv_v2):
    import jax
    import jax.numpy as jnp
    def _L0_conv_ref(x, Wq, bq, Wk, bk, Wv, bv, gamma):
        import jax, jax.numpy as jnp
        import numpy as np
        C = 256
        CK = C // 8
        B, Cc, H, W = x.shape
        xf = x.reshape(B, Cc, H * W)
        f = jnp.einsum('kc,bcn->bkn', Wq, xf) + bq[None, :, None]
        g = jnp.einsum('kc,bcn->bkn', Wk, xf) + bk[None, :, None]
        h = jnp.einsum('oc,bcn->bon', Wv, xf) + bv[None, :, None]
        s = jnp.einsum('bki,bkj->bij', f, g)
        beta = jax.nn.softmax(s, axis=1)
        o = jnp.einsum('bci,bij->bcj', h, beta)
        o = gamma[0] * o
        return o.reshape(B, Cc, H, W)

    def _L1_conv_ref(x, w1, b1, g1, be1, m1, v1, w2, b2, g2, be2, m2, v2):
        import jax, jax.numpy as jnp
        import numpy as np
        C_MID = 32
        _ROWS = np.concatenate([np.arange(C_MID - i) + i for i in range(C_MID)])
        _COLS = np.concatenate([np.arange(C_MID - i) for i in range(C_MID)])

        def _bn_relu(y, g, b, m, v, eps=1e-05):
            inv = g / jnp.sqrt(v + eps)
            return jax.nn.relu(y * inv[:, None, None] + (b - m * inv)[:, None, None])
        y = jnp.einsum('bchw,oc->bohw', x, w1) + b1[:, None, None]
        y = _bn_relu(y, g1, be1, m1, v1)
        yb = jnp.transpose(y, (0, 2, 3, 1))
        rows = jnp.asarray(_ROWS)
        cols = jnp.asarray(_COLS)
        packed = yb[..., rows] * yb[..., cols]
        z = jnp.einsum('bhwt,ot->bohw', packed, w2) + b2[:, None, None]
        return _bn_relu(z, g2, be2, m2, v2)

    def _gn(v, G=32, eps=1e-5):
        B_, C_, H_, W_ = v.shape
        g = v.reshape(B_, G, C_ // G, H_, W_)
        m = jnp.mean(g, axis=(2, 3, 4), keepdims=True)
        s = jnp.var(g, axis=(2, 3, 4), keepdims=True)
        return ((g - m) / jnp.sqrt(s + eps)).reshape(v.shape)

    def _ln_c(v, eps=1e-6):
        m = jnp.mean(v, axis=1, keepdims=True)
        s = jnp.var(v, axis=1, keepdims=True)
        return (v - m) / jnp.sqrt(s + eps)

    def _ln_t(v, eps=1e-5):
        m = jnp.mean(v, axis=-1, keepdims=True)
        s = jnp.var(v, axis=-1, keepdims=True)
        return (v - m) / jnp.sqrt(s + eps)

    def _to_tokens(v):
        B_, C_, H_, W_ = v.shape
        return v.reshape(B_, C_, H_ * W_).transpose(0, 2, 1)
    def _from_tokens(t, like):
        B_, C_, H_, W_ = like.shape
        return t.transpose(0, 2, 1).reshape(B_, C_, H_, W_)

    x = x + _L0_conv_ref(_gn(x), L0_conv_Wq, L0_conv_bq, L0_conv_Wk, L0_conv_bk, L0_conv_Wv, L0_conv_bv, L0_conv_gamma)
    x = x + _L1_conv_ref(_gn(x), L1_conv_w1, L1_conv_b1, L1_conv_g1, L1_conv_be1, L1_conv_m1, L1_conv_v1, L1_conv_w2, L1_conv_b2, L1_conv_g2, L1_conv_be2, L1_conv_m2, L1_conv_v2)
    return x


_drawn_inputs = setup_inputs


def setup_inputs(seed=0):
    import zlib

    import numpy as np

    out = dict(_drawn_inputs(seed))
    spreads = {}
    factors = {}
    for name, (base, spread) in spreads.items():
        noise = np.random.default_rng([zlib.crc32(name.encode()), seed]).standard_normal(out[name].shape)
        drawn = base * np.exp(spread * noise) if base else spread * noise
        out[name] = jnp.asarray(drawn.astype(out[name].dtype))
    for name, factor in factors.items():
        out[name] = (out[name] * factor).astype(out[name].dtype)
    return out
```

```python
from contextlib import ExitStack

import concourse.bass as bass
from concourse import mybir

B, C, HW = 4, 256, 4096
CK = C // 8
MID = 32
PAIRS = MID * (MID + 1) // 2
P = 128
CH = 512
NCH = HW // CH
NT = HW // P
QT = CH // P
H2 = C // P
GROUP = 8
REM = PAIRS - 4 * P
W2C = 4 * P + 96
GN_EPS = 1e-5
BN_EPS = 1e-5
GN_MAX = 182.0
TINY = 1e-30
F16_TOP = 2.0 ** 15
QK_TOP = 2.0 ** 14
M_ROWS = (2.0 ** 14, 2.0 ** 3, 2.0 ** -8)
LO = 2.0 ** 11
EXP_SHIFT = 8.0
SLOTS = 4
LEAD = 5

V_BQ, V_BK, V_BV, V_GAMMA, V_B1, V_G1, V_BE1, V_M1, V_V1 = 0, 1, 2, 4, 5, 6, 7, 8, 9
V_B2, V_G2, V_BE2, V_M2, V_V2, V_FROW, V_N = 10, 12, 14, 16, 18, 20, 21


def build(nc, x, wq, wk, wv, w1, w2, vec, ident, gmean, sel, out):
    f32, f16 = mybir.dt.float32, mybir.dt.float16
    ACT = mybir.ActivationFunctionType
    ALU = mybir.AluOpType
    AX = mybir.AxisListType.X
    ds = bass.ds
    ctx = ExitStack()
    with ctx:
        def sb(name, shape, dt):
            return ctx.enter_context(nc.sbuf_tensor(name, shape, dt))

        def sem(name):
            return ctx.enter_context(nc.semaphore(name))

        xs = sb("xs", [P, H2, HW], f32)
        xh = sb("xh", [P, H2, HW], f16)
        xl = sb("xl", [P, H2, HW], f16)
        xn = sb("xn", [P, 2, H2, CH], f32)
        fst = sb("fst", [P, HW], f16)
        gst = sb("gst", [P, HW], f16)
        hth = sb("hth", [P, NT, C + 1], f16)
        htl = sb("htl", [P, NT, C], f16)
        p32 = sb("p32", [P, SLOTS, CH], f32)
        ph = sb("ph", [P, SLOTS, CH], f16)
        pl = sb("pl", [P, SLOTS, CH], f16)
        mx = sb("mx", [P, NT, NCH], f32)
        nm = sb("nm", [P, QT], f32)
        mw = sb("mw", [P, 7, QT], f32)
        r1 = sb("r1", [P, 2, QT], f32)
        r2 = sb("r2", [P, QT], f32)
        r3 = sb("r3", [P, QT], f32)
        mrow = sb("mrow", [P, QT, P], f16)
        rinv = sb("rinv", [P, QT], f32)
        ot = sb("ot", [P, QT, C], f32)
        bst = sb("bst", [P, H2, NCH, 6], f32)
        bag = sb("bag", [P, H2, 2], f32)
        gin = sb("gin", [P, H2, 2], f32)
        gsb = sb("gsb", [P, H2, 2], f32)
        gmq = sb("gmq", [P, H2], f32)
        gve = sb("gve", [P, H2], f32)
        rstd = sb("rstd", [P, H2], f32)
        nbias = sb("nbias", [P, H2], f32)
        ybig = sb("ybig", [P, 2, CH], f32)
        yst = sb("yst", [64, 2, CH], f16)
        pb = sb("pb", [P, 5, CH], f32)
        qh = sb("qh", [P, 5, CH], f16)
        ql = sb("ql", [P, 4, CH], f16)
        zt = sb("zt", [P, 2, H2, CH], f32)
        og = sb("og", [P, 2, H2, CH], f32)
        wqn = sb("wqn", [96, C], f32)
        wkn = sb("wkn", [96, C], f32)
        wvn = zt[:, 0, :, 0:C]
        w1n = sb("w1n", [P, C], f32)
        w2n = og[:].rearrange("p a h n -> p (a h n)")[:, 0:H2 * W2C].rearrange("p (h n) -> p h n", h=H2)
        vs = sb("vs", [P, V_N], f32)
        idn = sb("idn", [P, P], f32)
        idh = sb("idh", [P, P], f16)
        gm = sb("gm", [P, P], f32)
        ones = sb("ones", [P, P], f32)
        selh = sb("selh", [64, W2C], f16)
        wqT = sb("wqT", [P, 2, H2, 96], f16)
        wkT = sb("wkT", [P, 2, H2, 96], f16)
        wvT = sb("wvT", [P, 2, H2, C], f16)
        w1T = sb("w1T", [P, 2, H2, P], f16)
        w2T = sb("w2T", [P, 3, 4, C], f16)
        w2r = sb("w2r", [96, C], f16)
        sc = sb("sc", [P, 64], f32)
        exps = sb("exps", [P, 4], f32)
        spare = sb("spare", [P, 16], f32)
        bq = sb("bq", [96, 1], f32)
        bk = sb("bk", [96, 1], f32)
        esc = sb("esc", [P, 1], f32)
        vout = sb("vout", [P, H2], f32)
        gbv = sb("gbv", [P, H2], f32)
        s1a = sb("s1a", [P, 1], f32)
        t1a = sb("t1a", [P, 1], f32)
        sc2 = sb("sc2", [P, H2], f32)
        t2 = sb("t2", [P, H2], f32)

        acc = [ctx.enter_context(nc.psum_tensor(f"acc{i}", [P, CH], f32)) for i in range(QT)]
        sps = [ctx.enter_context(nc.psum_tensor(f"sps{i}", [P, CH], f32)) for i in range(2)]
        tps = [ctx.enter_context(nc.psum_tensor(f"tps{i}", [P, CH], f32)) for i in range(2)]

        w_in = sem("w_in")
        x_in = [sem(f"x_in{c}") for c in range(NCH)]
        st_ok = sem("st_ok")
        set_dve = sem("set_dve")
        set_pool = sem("set_pool")
        set_pe = sem("set_pe")
        set_act = sem("set_act")
        gn_dve = sem("gn_dve")
        gn_in = sem("gn_in")
        gn_pe = sem("gn_pe")
        gn_var = sem("gn_var")
        gn_pow = sem("gn_pow")
        gn_ok = sem("gn_ok")
        xh_ok = sem("xh_ok")
        xn_ok = sem("xn_ok")
        xl_ok = sem("xl_ok")
        f_mm, g_mm, h_mm = sem("f_mm"), sem("g_mm"), sem("h_mm")
        f_hi, g_hi, h_hi = sem("f_hi"), sem("g_hi"), sem("h_hi")
        f_lo, g_lo, h_lo = sem("f_lo"), sem("g_lo"), sem("h_lo")
        t_mm = sem("t_mm")
        t_free = sem("t_free")
        nm_ok = sem("nm_ok")
        m_pool = sem("m_pool")
        m_rows = sem("m_rows")
        m_mm = sem("m_mm")
        m_ok = sem("m_ok")
        s_mm = sem("s_mm")
        ph_ok, p32_ok, pl_ok = sem("ph_ok"), sem("p32_ok"), sem("pl_ok")
        p_free = sem("p_free")
        acc_mm = sem("acc_mm")
        rinv_ok = sem("rinv_ok")
        ot_act = sem("ot_act")
        ot_dve = sem("ot_dve")
        o_mm = sem("o_mm")
        x1_ok = sem("x1_ok")
        bv_ok = sem("bv_ok")
        y_mm, y_ok, yh_ok, yl_ok = sem("y_mm"), sem("y_ok"), sem("yh_ok"), sem("yl_ok")
        sel_mm = sem("sel_mm")
        pb_ok, qh_ok, ql_ok = sem("pb_ok"), sem("qh_ok"), sem("ql_ok")
        z_mm, z_ok = sem("z_mm"), sem("z_ok")
        res_ok = sem("res_ok")
        og_free = [sem("og_free0"), sem("og_free1")]
        block = ctx.enter_context(nc.Block())

        class Steps:

            def __init__(self, eng, s, base=0):
                self.eng, self.s, self.base, self.n = eng, s, base, 0

            def __call__(self, ins):
                ins.then_inc(self.s, 1)
                self.n += 1
                self.eng.wait_ge(self.s, self.base + self.n)

        SPLITS = NT - QT + 1
        NLOADS = 9
        GN_STEPS = 7
        M_STEPS = 7

        xv = x.rearrange("b (h p) n -> b p h n", p=P)
        ov = out.rearrange("b (h p) n -> b p h n", p=P)
        R_BANK = [acc[1], acc[2], acc[3], tps[0], tps[1]]
        Y_BANK = acc[0]
        Z_BANK = sps

        (K_NQ, K_NK, K_PR, K_SUM, K_C2, K_A, K_BB, K_T, K_RS1, K_INV1, K_T1, K_YB, K_A2, K_AA, K_IA) = range(15)
        K_RV, K_RW, K_INV2, K_MX, K_U, K_W = 16, 18, 20, 22, 24, 26
        mark = {}

        def h_bank(c, k):
            return acc[2 * (c % 2) + k]

        @block.sync
        def _(sp):
            for dst, src in ((vs[:], vec), (wqn[:], wq), (wkn[:], wk), (wvn, wv), (w1n[:], w1), (w2n, w2), (idn[:], ident),
                             (gm[:], gmean), (selh[:], sel)):
                sp.dma_start(dst, src).then_inc(w_in, 16)
            for c in range(NCH):
                sp.dma_start(xs[:, :, c * CH:(c + 1) * CH], xv[0, :, :, c * CH:(c + 1) * CH]).then_inc(x_in[c], 16)

            def store(b, c):
                sp.wait_ge(res_ok, b * NCH + c + 1)
                sp.dma_start(ov[ds(b, 1), :, :, c * CH:(c + 1) * CH].rearrange("a p h n -> (a p) h n"),
                             og[:, c % 2]).then_inc(og_free[c % 2], 16)

            with sp.Fori(0, B - 1) as b:
                for c in range(NCH):
                    store(b, c)
                    sp.dma_start(xs[:, :, c * CH:(c + 1) * CH],
                                 xv[ds(b + 1, 1), :, :, c * CH:(c + 1) * CH].rearrange("a p h n -> (a p) h n")
                                 ).then_inc(x_in[c], 16)
            for c in range(NCH):
                store(B - 1, c)
            for par in range(2):
                sp.wait_ge(og_free[par], 16 * (B * NCH // 2 + 1))

        @block.vector
        def _(dve):
            V = nc.vector
            s = Steps(dve, set_dve)

            def col(k, n=1, p=P):
                return sc[0:p, k:k + n]

            def vc(k, n=1, p=P):
                return vs[0:p, k:k + n]

            carried = [0]

            def carry_wait():
                carried[0] = (carried[0] + 1) % 16
                V.memset(spare[:, carried[0]:carried[0] + 1], 0.0)

            def magnitude(o, v, least):
                s(V.scalar_tensor_tensor(o, v, -1.0, v, ALU.mult, ALU.max))
                s(V.tensor_scalar(o, o, least, None, ALU.add))

            s(V.memset(gst[96:P, :], 0.0))
            mark["zeros"] = s.n
            dve.wait_ge(w_in, 16 * NLOADS)
            dve.wait_ge(set_pool, 1)
            s(V.tensor_scalar(col(K_W), vc(V_V1), BN_EPS, None, ALU.add))
            s(V.tensor_scalar(col(K_W + 1, 2), vc(V_V2, 2), BN_EPS, None, ALU.add))
            mark["variances"] = s.n
            s(V.tensor_copy(idh[:], idn[:]))
            s(V.tensor_reduce(col(K_NQ, 1, 96), wqn[:], AX, ALU.add, apply_absolute_value=True))
            s(V.tensor_reduce(col(K_NK, 1, 96), wkn[:], AX, ALU.add, apply_absolute_value=True))
            magnitude(col(K_U, 2, 96), vc(V_BQ, 2, 96), TINY)
            s(V.tensor_tensor(col(K_NQ, 2, 96), col(K_NQ, 2, 96), col(K_U, 2, 96), ALU.add))
            s(V.tensor_tensor(col(K_PR, 1, 96), col(K_NQ, 1, 96), col(K_NK, 1, 96), ALU.mult))
            mark["bounds"] = s.n
            dve.wait_ge(set_pe, 1)
            s(V.tensor_scalar(esc[:], acc[0][:, 0:1], GN_MAX ** 2 / QK_TOP ** 2, None, ALU.mult))
            s(V.reciprocal(col(K_C2), esc[:]))
            s(V.reciprocal(col(K_BB, 1, 96), col(K_NQ, 1, 96)))
            s(V.scalar_tensor_tensor(col(K_T, 1, 96), col(K_NK, 1, 96), col(K_C2, 1, 96), col(K_BB, 1, 96),
                                     ALU.mult, ALU.mult))
            mark["ratio"] = s.n
            dve.wait_ge(set_pool, 3)
            s(V.reciprocal(col(K_T, 1, 96), col(K_A, 1, 96)))
            s(V.tensor_tensor(col(K_BB, 1, 96), col(K_T, 1, 96), col(K_C2, 1, 96), ALU.mult))
            s(V.tensor_scalar(wqn[:], wqn[:], col(K_A, 1, 96), None, ALU.mult))
            s(V.tensor_scalar(wkn[:], wkn[:], col(K_BB, 1, 96), None, ALU.mult))
            s(V.tensor_tensor(bq[:], vc(V_BQ, 1, 96), col(K_A, 1, 96), ALU.mult))
            s(V.tensor_tensor(bk[:], vc(V_BK, 1, 96), col(K_BB, 1, 96), ALU.mult))
            s(V.tensor_reduce(col(K_RV, 2), wvn, AX, ALU.add, apply_absolute_value=True))
            s(V.tensor_scalar(col(K_RV, 2), col(K_RV, 2), TINY, GN_MAX / F16_TOP, ALU.add, ALU.mult))
            s(V.reciprocal(col(K_RW, 2), col(K_RV, 2)))
            for h in range(H2):
                s(V.tensor_scalar(wvn[:, h], wvn[:, h], col(K_RW + h), None, ALU.mult))
            s(V.tensor_scalar(vout[:], col(K_RV, 2), vc(V_GAMMA), None, ALU.mult))
            s(V.tensor_scalar(gbv[:], vc(V_BV, 2), vc(V_GAMMA), None, ALU.mult))
            s(V.tensor_tensor(col(K_INV1), vc(V_G1), col(K_W), ALU.mult))
            s(V.tensor_reduce(col(K_RS1), w1n[:], AX, ALU.add, apply_absolute_value=True))
            s(V.tensor_tensor(col(K_T1), vc(V_B1), vc(V_M1), ALU.subtract))
            s(V.scalar_tensor_tensor(col(K_T1), col(K_T1), col(K_INV1), vc(V_BE1), ALU.mult, ALU.add))
            s(V.tensor_tensor(col(K_YB), col(K_RS1), col(K_INV1), ALU.mult))
            magnitude(col(K_T), col(K_YB), 0.0)
            s(V.tensor_scalar(col(K_YB), col(K_T), GN_MAX, None, ALU.mult))
            magnitude(col(K_U), col(K_T1), 1e-15)
            s(V.tensor_tensor(col(K_YB), col(K_YB), col(K_U), ALU.add))
            s(V.tensor_tensor(col(K_YB), col(K_YB), col(K_YB), ALU.mult))
            mark["squares"] = s.n
            dve.wait_ge(set_pe, 2)
            s(V.tensor_scalar(col(K_T), acc[1][:, 0:1], 1.0 / F16_TOP, None, ALU.mult))
            s(V.reciprocal(col(K_A2), col(K_T)))
            mark["square"] = s.n
            dve.wait_ge(set_pool, 4)
            s(V.tensor_tensor(col(K_T), col(K_AA), col(K_AA), ALU.mult))
            s(V.reciprocal(col(K_IA), col(K_T)))
            s(V.tensor_scalar(col(K_RS1), col(K_RS1), TINY, 2.0 ** -7, ALU.add, ALU.mult))
            s(V.reciprocal(col(K_U), col(K_RS1)))
            s(V.tensor_scalar(w1n[:], w1n[:], col(K_U), None, ALU.mult))
            s(V.tensor_scalar(col(K_AA), col(K_AA), LO, None, ALU.mult))
            s(V.tensor_tensor(col(K_T), col(K_INV1), col(K_RS1), ALU.mult))
            s(V.tensor_tensor(s1a[:], col(K_T), col(K_AA), ALU.mult))
            s(V.tensor_tensor(t1a[:], col(K_T1), col(K_AA), ALU.mult))
            s(V.tensor_reduce(col(K_MX, 2), w2n, AX, ALU.max, apply_absolute_value=True))
            s(V.tensor_scalar(col(K_MX, 2), col(K_MX, 2), TINY, 2.0 ** -14, ALU.add, ALU.mult))
            s(V.reciprocal(col(K_U, 2), col(K_MX, 2)))
            for h in range(H2):
                s(V.tensor_scalar(w2n[:, h], w2n[:, h], col(K_U + h), None, ALU.mult))
            s(V.tensor_tensor(col(K_INV2, 2), vc(V_G2, 2), col(K_W + 1, 2), ALU.mult))
            s(V.tensor_tensor(t2[:], vc(V_B2, 2), vc(V_M2, 2), ALU.subtract))
            s(V.tensor_tensor(t2[:], t2[:], col(K_INV2, 2), ALU.mult))
            s(V.tensor_tensor(t2[:], t2[:], vc(V_BE2, 2), ALU.add))
            s(V.tensor_tensor(col(K_INV2, 2), col(K_INV2, 2), col(K_MX, 2), ALU.mult))
            s(V.tensor_scalar(sc2[:], col(K_INV2, 2), col(K_IA), None, ALU.mult))
            s(V.tensor_scalar(mw[:, 6], mw[:, 0], 0.0, col(K_C2), ALU.mult, ALU.add))
            s(V.tensor_scalar(mw[:, 6], mw[:, 6], EXP_SHIFT, None, ALU.mult))
            mark["scaled"] = s.n
            dve.wait_ge(set_act, 1)
            V.tensor_tensor(wqT[:, 1], acc[0][:, 0:192].rearrange("p (h c) -> p h c", h=2), wqT[:, 0], ALU.subtract)
            V.tensor_tensor(wkT[:, 1], acc[1][:, 0:192].rearrange("p (h c) -> p h c", h=2), wkT[:, 0], ALU.subtract)
            V.tensor_tensor(wvT[:, 1], acc[2][:].rearrange("p (h c) -> p h c", h=2), wvT[:, 0], ALU.subtract)
            V.tensor_tensor(w1T[:, 1], acc[3][:, 0:256].rearrange("p (h c) -> p h c", h=2), w1T[:, 0], ALU.subtract)
            V.tensor_tensor(w2T[:, 1, 0:2], sps[0][:].rearrange("p (g c) -> p g c", g=2), w2T[:, 0, 0:2], ALU.subtract)
            V.tensor_tensor(w2T[:, 1, 2:4], sps[1][:].rearrange("p (g c) -> p g c", g=2), w2T[:, 0, 2:4], ALU.subtract)
            s(V.tensor_tensor(w2r[32:64, :], tps[0][32:64, 0:C], w2r[32:64, :], ALU.subtract))
            mark["weights"] = s.n

            def moments(n):
                g = Steps(dve, gn_dve, n * GN_STEPS)
                dve.wait_ge(st_ok, n + 1)
                carry_wait()
                for h in range(H2):
                    last = V.bn_aggr(bag[:, h], bst[:, h].rearrange("p c k -> p (c k)"))
                g(last)
                g(V.tensor_tensor(gmq[:], bag[:, :, 0], bag[:, :, 0], ALU.mult))
                g(V.tensor_copy(gin[:, :, 0], bag[:, :, 0]))
                V.tensor_tensor(gin[:, :, 1], bag[:, :, 1], gmq[:], ALU.add).then_inc(gn_in, 1)
                dve.wait_ge(gn_pe, n + 1)
                g(V.tensor_copy(gsb[:].rearrange("p h k -> p (h k)"), sps[0][:, 0:4]))
                g(V.tensor_tensor(gmq[:], gsb[:, :, 0], gsb[:, :, 0], ALU.mult))
                g(V.tensor_tensor(gve[:], gsb[:, :, 1], gmq[:], ALU.subtract))
                g(V.tensor_scalar(gve[:], gve[:], 0.0, GN_EPS, ALU.max, ALU.add))
                V.tensor_copy(nbias[:], gsb[:, :, 0]).then_inc(gn_var, 1)
                dve.wait_ge(gn_pow, n + 1)
                dve.wait_ge(gn_var, n + 1)
                V.scalar_tensor_tensor(nbias[:], gsb[:, :, 0], -1.0, rstd[:], ALU.mult, ALU.mult).then_inc(gn_ok, 1)
                dve.wait_ge(gn_ok, n + 1)

            def normed(n, par, at):
                dve.wait_ge(xl_ok, n + 1)
                for h in range(H2):
                    last = V.tensor_scalar(xn[:, par, h], xs[:, h, at], rstd[:, h:h + 1], nbias[:, h:h + 1],
                                           ALU.mult, ALU.add)
                last.then_inc(xn_ok, 1)

            def project_low(n, c):
                at = slice(c * CH, (c + 1) * CH)
                dve.wait_ge(f_hi, n + 1)
                V.scalar_tensor_tensor(fst[64:96, at], sps[0][64:96, :], bq[64:96], fst[64:96, at],
                                       ALU.add, ALU.subtract).then_inc(f_lo, 1)
                dve.wait_ge(g_hi, n + 1)
                V.scalar_tensor_tensor(gst[32:64, at], sps[1][32:64, :], bk[32:64], gst[32:64, at],
                                       ALU.add, ALU.subtract).then_inc(g_lo, 1)
                for k in range(2):
                    dve.wait_ge(h_hi, 2 * n + k + 1)
                    t = c * QT + 2 * k
                    V.tensor_tensor(htl[:, t:t + 2], h_bank(c, k)[:].rearrange("p (t c) -> p t c", t=2),
                                    hth[:, t:t + 2, 0:C], ALU.subtract).then_inc(h_lo, 1)

            def piece_max(n, tile, c, par):
                dve.wait_ge(t_mm, n + 1)
                V.reduce_max(mx[:, ds(tile, 1), c], tps[par][:], AX).then_inc(t_free, 1)

            def tile_max(n, tile, k):
                dve.wait_ge(t_free, n + 2)
                carry_wait()
                V.tensor_reduce(nm[:, k:k + 1], mx[:, ds(tile, 1)], AX, ALU.max, negate=True).then_inc(nm_ok, 1)

            def finish_block(n, J, half_):
                dve.wait_ge(o_mm, 2 * n + half_ + 1)
                at = ds(J * CH, CH)
                V.scalar_tensor_tensor(xs[:, half_, at], tps[1 - half_][:], vout[:, half_:half_ + 1],
                                       xs[:, half_, at], ALU.mult, ALU.add).then_inc(x1_ok, 1)

            def stats(n, J, half_):
                dve.wait_ge(x1_ok, 2 * n + half_ + 1)
                return V.bn_stats(bst[:, half_, ds(J, 1)].rearrange("p a k -> p (a k)"), xs[:, half_, ds(J * CH, CH)])

            def divide(b, J):
                n = b * NCH + J
                for j in range(QT):
                    if j + 1 < QT:
                        dve.wait_ge(acc_mm, n * (QT - 1) + j + 1)
                    else:
                        dve.wait_ge(p_free, SLOTS + (n + 1) * NT)
                    V.reciprocal(rinv[:, j:j + 1], acc[j][:, C:C + 1]).then_inc(rinv_ok, 1)
                for j in (2, 3):
                    dve.wait_ge(rinv_ok, n * QT + j + 1)
                    V.tensor_scalar(ot[:, j], acc[j][:, 0:C], rinv[:, j:j + 1], None, ALU.mult).then_inc(ot_dve, 1)

            def group(b, J, q, maxima=True, finish=False):
                k = J * QT + q
                T = b * (NT * NCH) + J * NT + q * 8
                N = b * (NT * NCH) + (k + LEAD) * 8
                for u in range(8):
                    dve.wait_ge(p32_ok, T + u + 1)
                    V.tensor_tensor(pl[:, u % SLOTS], p32[:, u % SLOTS], ph[:, u % SLOTS],
                                    ALU.subtract).then_inc(pl_ok, 1)
                    if finish and u == 0:
                        divide(b, J - 1)
                    if finish and u in (1, 2):
                        if u == 1:
                            dve.wait_ge(bv_ok, b + 1)
                        finish_block(b * NCH + J - 1, J - 1, u - 1)
                    if finish and u in (2, 3):
                        stats(b * NCH + J - 1, J - 1, u - 2)
                    if maxima:
                        piece_max(N + u, k + LEAD, u, u % 2)
                if maxima:
                    tile_max(N + 8, k + LEAD, (q + LEAD) % QT)

            def products(n, g, par):
                rows = P if g < 4 else 96
                dve.wait_ge(sel_mm, 5 * n + g + 1)
                dve.wait_ge(y_ok, n + 1)
                V.tensor_tensor(pb[0:rows, g], ybig[0:rows, par], R_BANK[g][0:rows, :],
                                ALU.mult).then_inc(pb_ok, 1)

            def product_low(n, g):
                dve.wait_ge(qh_ok, 5 * n + g + 1)
                if g < 4:
                    V.scalar_tensor_tensor(ql[:, g], qh[:, g], -LO, pb[:, g], ALU.mult,
                                           ALU.add).then_inc(ql_ok, 1)
                else:
                    V.scalar_tensor_tensor(qh[64:96, g], qh[64:96, g], -LO, pb[64:96, g], ALU.mult,
                                           ALU.add).then_inc(ql_ok, 1)

            def y_low(n, par):
                dve.wait_ge(yh_ok, n + 1)
                V.scalar_tensor_tensor(yst[32:64, par], yst[32:64, par], -LO, ybig[32:64, par], ALU.mult,
                                       ALU.add).then_inc(yl_ok, 1)

            with dve.Fori(0, B) as b:
                nb = b * (2 * NCH)
                for c in range(NCH):
                    dve.wait_ge(x_in[c], 16 * (b + 1))
                    for h in range(H2):
                        last = V.bn_stats(bst[:, h, c], xs[:, h, c * CH:(c + 1) * CH])
                last.then_inc(st_ok, 1)
                moments(b * 2)
                for c in range(2):
                    normed(nb + c, c, slice(c * CH, (c + 1) * CH))
                for c in range(NCH):
                    if c + 2 < NCH:
                        normed(nb + c + 2, c % 2, slice((c + 2) * CH, (c + 3) * CH))
                    project_low(b * NCH + c, c)
                    if c:
                        for t in range(LEAD):
                            piece_max(b * (NT * NCH) + (c - 1) * LEAD + t, t, c - 1, ((c - 1) * LEAD + t) % 2)
                for t in range(LEAD):
                    piece_max(b * (NT * NCH) + (NCH - 1) * LEAD + t, t, NCH - 1, ((NCH - 1) * LEAD + t) % 2)
                dve.wait_ge(t_free, b * (NT * NCH) + NCH * LEAD + 2)
                carry_wait()
                V.tensor_reduce(nm[:, 0:QT], mx[:, 0:QT], AX, ALU.max, negate=True).then_inc(nm_ok, QT)
                for t in range(QT, LEAD):
                    dve.wait_ge(m_rows, b * NT + t - QT + 1)
                    tile_max(b * (NT * NCH) + NCH * LEAD, t, t % QT)
                group(b, 0, 0)
                with dve.Fori(0, NCH - 2) as J:
                    for q in (1, 2, 3):
                        group(b, J, q)
                    group(b, J + 1, 0, finish=True)
                for q in (1, 2):
                    group(b, NCH - 2, q)
                group(b, NCH - 2, 3, maxima=False)
                group(b, NCH - 1, 0, maxima=False, finish=True)
                for q in (1, 2, 3):
                    group(b, NCH - 1, q, maxima=False)
                divide(b, NCH - 1)
                for h in range(H2):
                    finish_block(b * NCH + NCH - 1, NCH - 1, h)
                for h in range(H2):
                    last = stats(b * NCH + NCH - 1, NCH - 1, h)
                last.then_inc(st_ok, 1)
                moments(b * 2 + 1)
                for c in range(3):
                    normed(nb + NCH + c, c % 2, slice(c * CH, (c + 1) * CH))
                y_low(b * NCH, 0)
                for c in range(NCH):
                    n = b * NCH + c
                    products(n, 0, c % 2)
                    products(n, 1, c % 2)
                    product_low(n, 0)
                    products(n, 2, c % 2)
                    product_low(n, 1)
                    if c + 1 < NCH:
                        y_low(n + 1, (c + 1) % 2)
                    products(n, 3, c % 2)
                    product_low(n, 2)
                    products(n, 4, c % 2)
                    product_low(n, 3)
                    product_low(n, 4)
                    if c + 3 < NCH:
                        normed(nb + NCH + c + 3, (c + 3) % 2, slice((c + 3) * CH, (c + 4) * CH))
        @block.gpsimd
        def _(pool):
            nc.gpsimd.memset(exps[:, 0:3], -0.5).then_inc(xl_ok, 2)
            nc.gpsimd.memset(exps[:, 3:4], 0.5).then_inc(t_free, 2)
            nc.gpsimd.memset(mrow[:, 0:1], 0.0).then_inc(p_free, SLOTS)
            nc.gpsimd.memset(mrow[:, 1:2], 0.0).then_inc(ot_act, 2)
            nc.gpsimd.memset(ones[:, 0:P // 4], 1.0).then_inc(ot_dve, 2)
            nc.gpsimd.memset(mrow[:, 2:QT], 0.0).then_inc(m_ok, QT)
            nc.gpsimd.memset(hth[:, :, C:C + 1], 1.0).then_inc(og_free[0], 16)
            nc.gpsimd.memset(ones[:, P // 4:P // 2], 1.0).then_inc(og_free[1], 16)
            for i in range(3):
                nc.gpsimd.memset(mw[:, i], M_ROWS[i])
                nc.gpsimd.memset(mw[:, 3 + i], 1 / M_ROWS[i])
            nc.gpsimd.memset(ones[:, P // 2:], 1.0).then_inc(set_pool, 1)
            pool.wait_ge(set_pool, 1)
            pool.wait_ge(set_dve, mark["variances"])
            nc.gpsimd.tensor_tensor(sc[:, K_W:K_W + 3], sc[:, K_W:K_W + 3], exps[:, 0:3],
                                    ALU.pow).then_inc(set_pool, 1)
            pool.wait_ge(set_dve, mark["ratio"])
            nc.gpsimd.tensor_tensor(sc[0:96, K_A:K_A + 1], sc[0:96, K_T:K_T + 1], exps[0:96, 3:4],
                                    ALU.pow).then_inc(set_pool, 1)
            pool.wait_ge(set_dve, mark["square"])
            nc.gpsimd.tensor_tensor(sc[:, K_AA:K_AA + 1], sc[:, K_A2:K_A2 + 1], exps[:, 3:4],
                                    ALU.pow).then_inc(set_pool, 1)

            def power(n):
                pool.wait_ge(gn_var, n)
                nc.gpsimd.tensor_tensor(rstd[:], gve[:], exps[:, 0:2], ALU.pow).then_inc(gn_pow, 1)

            def low(n, c, at):
                pool.wait_ge(xh_ok, n + c + 1)
                pool.wait_ge(xn_ok, n + c + 1)
                for h in range(H2):
                    last = nc.gpsimd.tensor_tensor(xl[:, h, at], xn[:, c % 2, h], xh[:, h, at], ALU.subtract)
                last.then_inc(xl_ok, 1)

            def split_max(n, k, splits):
                pool.wait_ge(nm_ok, n + 1)
                pool.wait_ge(m_ok, n + 1)
                wide = k.stop - k.start
                step = Steps(pool, m_pool, splits * M_STEPS)
                tt = nc.gpsimd.tensor_tensor

                def wt(i):
                    return mw[:, i, 0:wide]

                step(tt(r3[:, k], nm[:, k], wt(6), ALU.add))
                rest_ = r3[:, k]
                for i in range(3):
                    part = mrow[:, k, 96 + i]
                    ins = tt(part, rest_, wt(3 + i), ALU.mult)
                    if i == 2:
                        ins.then_inc(m_rows, wide)
                        break
                    step(ins)
                    step(tt(r2[:, k], part, wt(i), ALU.mult))
                    step(tt(r1[:, i, k], rest_, r2[:, k], ALU.subtract))
                    rest_ = r1[:, i, k]

            def residual(b, c):
                pool.wait_ge(z_ok, 2 * (b * NCH + c + 1))
                pool.wait_ge(og_free[c % 2], 16 * (b * (NCH // 2) + c // 2 + 1))
                for h in range(H2):
                    last = nc.gpsimd.tensor_tensor(og[:, c % 2, h], xs[:, h, c * CH:(c + 1) * CH],
                                                   zt[:, c % 2, h], ALU.add)
                last.then_inc(res_ok, 1)

            with pool.Fori(0, B) as b:
                power(b * 2 + 1)
                for c in range(NCH):
                    low(b * (2 * NCH), c, slice(c * CH, (c + 1) * CH))
                pool.wait_ge(set_pool, 1)
                pool.wait_ge(xh_ok, b * (2 * NCH) + NCH)
                pool.wait_ge(xn_ok, b * (2 * NCH) + NCH)
                for h in range(H2):
                    last = nc.gpsimd.tensor_scalar(xs[:, h], xs[:, h], 1.0, gbv[:, h:h + 1], ALU.mult, ALU.add)
                last.then_inc(bv_ok, 1)
                split_max(b * NT + QT - 1, slice(0, QT), b * SPLITS)
                with pool.Fori(1, NT // QT) as jj:
                    for u in range(QT):
                        split_max(b * NT + jj * QT + u, slice(u, u + 1), b * SPLITS + 1 - QT + jj * QT + u)
                power(b * 2 + 2)
                for c in range(3):
                    low(b * (2 * NCH) + NCH, c, slice(c * CH, (c + 1) * CH))
                for c in range(NCH):
                    if c + 3 < NCH:
                        low(b * (2 * NCH) + NCH, c + 3, slice((c + 3) * CH, (c + 4) * CH))
                    residual(b, c)


        @block.scalar
        def _(act):
            A = nc.scalar.activation
            act.wait_ge(set_pool, 1)
            act.wait_ge(set_dve, mark["zeros"])
            act.wait_ge(w_in, 16 * NLOADS)
            A(fst[96:P, :], gst[96:P, :], ACT.Identity, bias=vs[96:P, V_FROW:V_FROW + 1])
            act.wait_ge(set_pe, 3)
            A(wqT[:, 0], acc[0][:, 0:192].rearrange("p (h c) -> p h c", h=2), ACT.Copy)
            A(wkT[:, 0], acc[1][:, 0:192].rearrange("p (h c) -> p h c", h=2), ACT.Copy)
            A(wvT[:, 0], acc[2][:].rearrange("p (h c) -> p h c", h=2), ACT.Copy)
            A(w1T[:, 0], acc[3][:, 0:256].rearrange("p (h c) -> p h c", h=2), ACT.Copy)
            A(w2T[:, 0, 0:2], sps[0][:].rearrange("p (g c) -> p g c", g=2), ACT.Copy)
            A(w2T[:, 0, 2:4], sps[1][:].rearrange("p (g c) -> p g c", g=2), ACT.Copy)
            A(w2r[:], tps[0][0:96, 0:C], ACT.Copy).then_inc(set_act, 1)
            act.wait_ge(set_act, 1)
            A(w2T[:, 2], w2T[:, 0], ACT.Copy, scale=1.0 / LO)
            A(w2r[64:96, :], w2r[64:96, :], ACT.Copy, scale=1.0 / LO).then_inc(set_act, 1)

            def high(at):
                for h in range(H2):
                    last = A(xh[:, h, at], xs[:, h, at], ACT.Identity, bias=nbias[:, h:h + 1],
                             scale=rstd[:, h:h + 1])
                last.then_inc(xh_ok, 1)

            def project_high(n, c):
                at = slice(c * CH, (c + 1) * CH)
                act.wait_ge(f_mm, n + 1)
                A(fst[0:96, at], sps[0][0:96, :], ACT.Identity, bias=bq[:]).then_inc(f_hi, 1)
                act.wait_ge(g_mm, n + 1)
                A(gst[0:96, at], sps[1][0:96, :], ACT.Identity, bias=bk[:]).then_inc(g_hi, 1)
                for k in range(2):
                    act.wait_ge(h_mm, 2 * n + k + 1)
                    t = c * QT + 2 * k
                    A(hth[:, t:t + 2, 0:C], h_bank(c, k)[:].rearrange("p (t c) -> p t c", t=2),
                      ACT.Copy).then_inc(h_hi, 1)

            def divide(b, J):
                for j in (0, 1):
                    act.wait_ge(rinv_ok, (b * NCH + J) * QT + j + 1)
                    A(ot[:, j], acc[j][:, 0:C], ACT.Copy, scale=rinv[:, j:j + 1]).then_inc(ot_act, 1)

            def group(b, J, q, rows=True, finish=False):
                k = J * QT + q
                T = b * (NT * NCH) + J * NT + q * 8
                for u in range(8):
                    act.wait_ge(s_mm, T + u + 1)
                    act.wait_ge(p_free, T + u + 1)
                    A(ph[:, u % SLOTS], sps[u % 2][:], ACT.Exp, scale=esc[:]).then_inc(ph_ok, 1)
                    A(p32[:, u % SLOTS], sps[u % 2][:], ACT.Exp, scale=esc[:]).then_inc(p32_ok, 1)
                    if finish and u == 1:
                        divide(b, J - 1)
                    if rows and u == 4:
                        act.wait_ge(m_mm, b * NT + k + LEAD)
                        A(gst[96:99, ds((k + LEAD - 1) * P, P)], tps[0][96:99, 0:P], ACT.Copy).then_inc(m_ok, 1)

            def y_high(n, par):
                act.wait_ge(y_mm, n + 1)
                A(ybig[:, par], Y_BANK[:], ACT.Relu, bias=t1a[:], scale=s1a[:]).then_inc(y_ok, 1)
                act.wait_ge(y_ok, n + 1)
                A(yst[:, par], ybig[0:64, par], ACT.Copy, scale=1.0 / LO).then_inc(yh_ok, 1)

            def product_high(n, g):
                rows = P if g < 4 else 96
                act.wait_ge(pb_ok, 5 * n + g + 1)
                A(qh[0:rows, g], pb[0:rows, g], ACT.Copy, scale=1.0 / LO).then_inc(qh_ok, 1)

            with act.Fori(0, B) as b:
                act.wait_ge(gn_ok, 2 * b + 1)
                for c in range(2):
                    high(slice(c * CH, (c + 1) * CH))
                for c in range(NCH):
                    if c + 2 < NCH:
                        high(slice((c + 2) * CH, (c + 3) * CH))
                    project_high(b * NCH + c, c)
                act.wait_ge(m_mm, b * NT + QT)
                A(gst[96:99, 0:CH], tps[0][96:99, :], ACT.Copy).then_inc(m_ok, QT)
                group(b, 0, 0)
                with act.Fori(0, NCH - 2) as J:
                    for q in (1, 2, 3):
                        group(b, J, q)
                    group(b, J + 1, 0, finish=True)
                for q in (1, 2, 3):
                    group(b, NCH - 2, q)
                group(b, NCH - 1, 0, rows=False, finish=True)
                for q in (1, 2, 3):
                    group(b, NCH - 1, q, rows=False)
                divide(b, NCH - 1)
                act.wait_ge(gn_ok, 2 * b + 2)
                for c in range(3):
                    high(slice(c * CH, (c + 1) * CH))
                y_high(b * NCH, 0)
                for c in range(NCH):
                    n = b * NCH + c
                    product_high(n, 0)
                    if c + 1 < NCH:
                        y_high(n + 1, (c + 1) % 2)
                    for g in range(1, 5):
                        product_high(n, g)
                    for h in range(H2):
                        act.wait_ge(z_mm, 2 * n + h + 1)
                        if c >= 2:
                            act.wait_ge(res_ok, n - 1)
                        A(zt[:, c % 2, h], Z_BANK[h][:], ACT.Relu, bias=t2[:, h:h + 1],
                          scale=sc2[:, h:h + 1]).then_inc(z_ok, 1)
                    if c + 3 < NCH:
                        high(slice((c + 3) * CH, (c + 4) * CH))

        @block.tensor
        def _(pe):
            mm = nc.tensor.matmul
            pe.wait_ge(w_in, 16 * NLOADS)
            pe.wait_ge(set_pool, 1)
            pe.wait_ge(set_dve, mark["bounds"])
            mm(acc[0][:, 0:1], ones[0:CK, :], sc[0:CK, K_PR:K_PR + 1], start=True, stop=True).then_inc(set_pe, 1)
            pe.wait_ge(set_dve, mark["squares"])
            mm(acc[1][:, 0:1], ones[0:MID, :], sc[0:MID, K_YB:K_YB + 1], start=True, stop=True).then_inc(set_pe, 1)
            pe.wait_ge(set_dve, mark["scaled"])
            tr = nc.tensor.transpose
            for i in range(H2):
                at = slice(i * P, (i + 1) * P)
                tr(acc[0][:, i * 96:(i + 1) * 96], wqn[:, at], idn[0:96, 0:96])
                tr(acc[1][:, i * 96:(i + 1) * 96], wkn[:, at], idn[0:96, 0:96])
                tr(acc[3][:, at], w1n[:, at], idn[:])
                for o in range(H2):
                    tr(acc[2][:, i * C + o * P:i * C + (o + 1) * P], wvn[:, o, at], idn[:])
                for g in range(4):
                    tr(sps[g // 2][:, (g % 2) * C + i * P:(g % 2) * C + (i + 1) * P],
                       w2n[:, i, g * P:(g + 1) * P], idn[:])
                last = tr(tps[0][0:96, i * P:(i + 1) * P], w2n[:, i, 4 * P:W2C], idn[:])
            last.then_inc(set_pe, 1)
            pe.wait_ge(set_act, 2)
            pe.wait_ge(set_dve, mark["weights"])

            def three(out, wT, at, cols):
                for i in range(H2):
                    for w, v in ((0, xh), (0, xl), (1, xh)):
                        last = mm(out, wT[:, w, i, cols], v[:, i, at], start=(i == 0 and w == 0 and v is xh),
                                  stop=(i == H2 - 1 and w == 1))
                return last

            def moments(n):
                pe.wait_ge(gn_in, n + 1)
                mm(sps[0][:, 0:4], gm[:], gin[:].rearrange("p h k -> p (h k)"), start=True,
                   stop=True).then_inc(gn_pe, 1)

            def project(b, c):
                n = b * NCH + c
                at = slice(c * CH, (c + 1) * CH)
                pe.wait_ge(xl_ok, b * (2 * NCH) + c + 3)
                if c:
                    pe.wait_ge(f_lo, n)
                three(sps[0][0:96, :], wqT, at, slice(0, 96)).then_inc(f_mm, 1)
                if c:
                    pe.wait_ge(g_lo, n)
                three(sps[1][0:96, :], wkT, at, slice(0, 96)).then_inc(g_mm, 1)
                for k in range(2):
                    if c >= 2:
                        pe.wait_ge(h_lo, 2 * (n - 2) + k + 1)
                    for e in range(2):
                        t = (c * QT + 2 * k + e) * P
                        for i in range(H2):
                            for w, v in ((0, xh), (1, xh), (0, xl)):
                                last = mm(h_bank(c, k)[:, e * C:(e + 1) * C], v[:, i, t:t + P], wvT[:, w, i],
                                          start=(i == 0 and w == 0 and v is xh), stop=(i == H2 - 1 and v is xl))
                    last.then_inc(h_mm, 1)

            def piece(n, tile, c, par):
                pe.wait_ge(t_free, n + 1)
                mm(tps[par][:], gst[0:96, ds(tile * P, P)], fst[0:96, c * CH:(c + 1) * CH], start=True,
                   stop=True).then_inc(t_mm, 1)

            def scores(T, tile, J, par, first=False):
                if not first:
                    pe.wait_ge(p32_ok, T - 1)
                mm(sps[par][:], fst[:, tile * P:(tile + 1) * P], gst[:, ds(J * CH, CH)], start=True,
                   stop=True).then_inc(s_mm, 1)

            def transposed(n, h):
                pe.wait_ge(ot_act, 2 * (n + 2))
                pe.wait_ge(ot_dve, 2 * (n + 2))
                for j in range(QT):
                    last = tr(tps[1 - h][:, j * P:(j + 1) * P], ot[:, j, h * P:(h + 1) * P], idn[:])
                last.then_inc(o_mm, 1)

            def group(b, J, q, maxima=True, rows=True, finish=False, end=False):
                k = J * QT + q
                T = b * (NT * NCH) + J * NT + q * 8
                N = b * (NT * NCH) + (k + LEAD) * 8
                for u in range(8):
                    t = q * 8 + u
                    if t + 2 < NT:
                        scores(T + u + 2, t + 2, J, u % 2)
                    elif not end:
                        if t + 2 == NT:
                            pe.wait_ge(m_ok, b * NT + (J + 2) * QT + QT)
                        scores(T + u + 2, t + 2 - NT, J + 1, u % 2)
                    if rows and u == 4:
                        tile = k + LEAD - 1
                        if maxima:
                            pe.wait_ge(t_free, N + u + 1)
                        pe.wait_ge(m_rows, b * NT + tile + 1)
                        mm(tps[0][:, 0:P], mrow[:, (q + LEAD - 1) % QT], idh[:], start=True,
                           stop=True).then_inc(m_mm, 1)
                    if finish and u in (1, 2):
                        n = b * NCH + J - 1
                        if maxima:
                            pe.wait_ge(t_free, N + u + 1)
                        transposed(n, u - 1)
                    slot = u % SLOTS
                    pe.wait_ge(ph_ok, T + u + 1)
                    for j in range(QT):
                        if t == 0:
                            pe.wait_ge(ot_act if j < 2 else ot_dve, (b * NCH + J) * 2 + j % 2 + 1)
                        w = ph[:, slot, j * P:(j + 1) * P]
                        mm(acc[j][:, 0:C + 1], w, hth[:, t], start=(t == 0), stop=False)
                        mm(acc[j][:, 0:C], w, htl[:, t], start=False, stop=False)
                    if rows and u == 4:
                        pe.wait_ge(m_ok, b * NT + tile + 1 + QT)
                    if finish and u in (1, 2):
                        pe.wait_ge(x1_ok, 2 * n + u)
                    if maxima:
                        piece(N + u, k + LEAD, u, u % 2)
                    pe.wait_ge(pl_ok, T + u + 1)
                    for j in range(QT):
                        last = mm(acc[j][:, 0:C + 1], pl[:, slot, j * P:(j + 1) * P], hth[:, t], start=False,
                                  stop=(t == NT - 1))
                        if t == NT - 1 and j + 1 < QT:
                            last.then_inc(acc_mm, 1)
                    last.then_inc(p_free, 1)

            def project_y(b, c):
                n = b * NCH + c
                pe.wait_ge(xl_ok, b * (2 * NCH) + NCH + c + 3)
                if c:
                    pe.wait_ge(y_ok, n)
                three(Y_BANK[:], w1T, slice(c * CH, (c + 1) * CH), slice(0, P)).then_inc(y_mm, 1)

            def select(n, par):
                pe.wait_ge(yl_ok, n + 1)
                for g in range(5):
                    cols = slice(g * P, min((g + 1) * P, W2C))
                    rows = P if g < 4 else 96
                    mm(R_BANK[g][0:rows, :], selh[:, cols], yst[:, par], start=True, stop=True).then_inc(sel_mm, 1)

            with pe.Fori(0, B) as b:
                moments(2 * b)
                for c in range(NCH):
                    project(b, c)
                    if c == 1:
                        pe.wait_ge(g_lo, b * NCH + 2)
                    if c:
                        pe.wait_ge(f_lo, b * NCH + c)
                        for t in range(LEAD):
                            i = (c - 1) * LEAD + t
                            piece(b * (NT * NCH) + i, t, c - 1, i % 2)
                pe.wait_ge(f_lo, b * NCH + NCH)
                for t in range(LEAD):
                    i = (NCH - 1) * LEAD + t
                    piece(b * (NT * NCH) + i, t, NCH - 1, i % 2)
                pe.wait_ge(t_free, b * (NT * NCH) + NCH * LEAD + 2)
                for t in range(QT):
                    pe.wait_ge(m_rows, b * NT + t + 1)
                    mm(tps[0][:, t * P:(t + 1) * P], mrow[:, t], idh[:], start=True, stop=True).then_inc(m_mm, 1)
                pe.wait_ge(m_ok, b * NT + 2 * QT)
                pe.wait_ge(g_lo, b * NCH + NCH)
                pe.wait_ge(h_lo, 2 * (b * NCH + NCH))
                for t in range(2):
                    scores(0, t, 0, t, first=True)
                group(b, 0, 0)
                with pe.Fori(0, NCH - 2) as J:
                    for q in (1, 2, 3):
                        group(b, J, q)
                    group(b, J + 1, 0, finish=True)
                for q in (1, 2):
                    group(b, NCH - 2, q)
                group(b, NCH - 2, 3, maxima=False)
                group(b, NCH - 1, 0, maxima=False, rows=False, finish=True)
                for q in (1, 2):
                    group(b, NCH - 1, q, maxima=False, rows=False)
                group(b, NCH - 1, 3, maxima=False, rows=False, end=True)
                for h in range(H2):
                    transposed(b * NCH + NCH - 1, h)
                moments(2 * b + 1)
                project_y(b, 0)
                select(b * NCH, 0)
                for c in range(NCH):
                    n = b * NCH + c
                    if c + 1 < NCH:
                        project_y(b, c + 1)
                    if c:
                        pe.wait_ge(z_ok, 2 * n)
                    for g in range(5):
                        pe.wait_ge(qh_ok, 5 * n + g + 1)
                        if g == 4:
                            pe.wait_ge(ql_ok, 5 * n + 5)
                            for h in range(H2):
                                mm(Z_BANK[h][:], w2r[:, h * P:(h + 1) * P], qh[0:96, 4], start=False,
                                   stop=True).then_inc(z_mm, 1)
                            continue
                        for h in range(H2):
                            for w in range(2):
                                mm(Z_BANK[h][:], w2T[:, w, g, h * P:(h + 1) * P], qh[:, g],
                                   start=(g == 0 and w == 0), stop=False)
                        pe.wait_ge(ql_ok, 5 * n + g + 1)
                        for h in range(H2):
                            mm(Z_BANK[h][:], w2T[:, 2, g, h * P:(h + 1) * P], ql[:, g], start=False, stop=False)
                    if c + 1 < NCH:
                        select(n + 1, (c + 1) % 2)
                pe.wait_ge(z_ok, 2 * (b * NCH + NCH))


def kernel(x, L0_conv_Wq, L0_conv_bq, L0_conv_Wk, L0_conv_bk, L0_conv_Wv, L0_conv_bv, L0_conv_gamma,
           L1_conv_w1, L1_conv_b1, L1_conv_g1, L1_conv_be1, L1_conv_m1, L1_conv_v1,
           L1_conv_w2, L1_conv_b2, L1_conv_g2, L1_conv_be2, L1_conv_m2, L1_conv_v2):
    import concourse.bacc as bacc
    import numpy as np
    from concourse.bass_utils import run_bass_kernel_spmd

    f = np.float32
    base = [sum(MID - e for e in range(d)) for d in range(MID + 1)]

    def column(i, c):
        lo, hi = sorted((c, (c + i) % MID))
        return base[hi - lo] + lo

    order = [column(i, c) for i in range(MID // 2) for c in range(MID)]
    rest = [column(MID // 2, c) for c in range(REM)]
    w2p = np.zeros((C, W2C), f)
    w2p[:, :4 * P] = np.asarray(L1_conv_w2)[:, order]
    sel = np.zeros((2 * MID, W2C), np.float16)
    for i in range(MID // 2):
        for c in range(MID):
            sel[(c + i) % MID, i * MID + c] = 1
            sel[MID + (c + i) % MID, i * MID + c] = 1 / LO
    for r in range(3):
        at = 4 * P + r * 32
        w2p[:, at:at + REM] = np.asarray(L1_conv_w2)[:, rest]
        for c in range(REM):
            sel[(c + MID // 2) % MID, at + c] = 1
            sel[MID + (c + MID // 2) % MID, at + c] = 1 / LO

    vec = np.zeros((P, V_N), f)
    for k, v in ((V_BQ, L0_conv_bq), (V_BK, L0_conv_bk)):
        vec[:96, k] = np.tile(np.asarray(v), 3)
    vec[:, V_GAMMA] = np.asarray(L0_conv_gamma)[0]
    for k, v in ((V_B1, L1_conv_b1), (V_G1, L1_conv_g1), (V_BE1, L1_conv_be1), (V_M1, L1_conv_m1),
                 (V_V1, L1_conv_v1)):
        vec[:, k] = np.tile(np.asarray(v), 4)
    for k, v in ((V_BV, L0_conv_bv), (V_B2, L1_conv_b2), (V_G2, L1_conv_g2), (V_BE2, L1_conv_be2),
                 (V_M2, L1_conv_m2), (V_V2, L1_conv_v2)):
        vec[:, k:k + 2] = np.asarray(v).reshape(2, P).T
    vec[96:99, V_FROW] = M_ROWS
    arrays = {
        "x": np.ascontiguousarray(np.asarray(x).reshape(B, C, HW)),
        "wq": np.tile(np.asarray(L0_conv_Wq), (3, 1)),
        "wk": np.tile(np.asarray(L0_conv_Wk), (3, 1)),
        "wv": np.ascontiguousarray(np.asarray(L0_conv_Wv).reshape(H2, P, C).transpose(1, 0, 2)),
        "w1": np.tile(np.asarray(L1_conv_w1), (4, 1)),
        "w2": np.ascontiguousarray(w2p.reshape(H2, P, W2C).transpose(1, 0, 2)),
        "vec": vec,
        "ident": np.eye(P, dtype=f),
        "gmean": np.kron(np.eye(P // GROUP, dtype=f), np.full((GROUP, GROUP), 1 / GROUP, f)),
        "sel": sel,
    }
    nc = bacc.Bacc("TRN2", target_bir_lowering=False, num_devices=1)
    args = [nc.dram_tensor(k, a.shape, mybir.dt.from_np(a.dtype), kind="ExternalInput").ap()
            for k, a in arrays.items()]
    args.append(nc.dram_tensor("out", (B, C, HW), mybir.dt.float32, kind="ExternalOutput").ap())
    build(nc, *args)
    r = run_bass_kernel_spmd(nc, [arrays], core_ids=[0])
    return r.results[0]["out"].reshape(B, C, 64, 64)
```

```python
from contextlib import ExitStack

import concourse.bass as bass
from concourse import mybir

B, C, HW = 4, 256, 4096
CK = C // 8
MID = 32
PAIRS = MID * (MID + 1) // 2
P = 128
CH = 512
NCH = HW // CH
NT = HW // P
QT = CH // P
H2 = C // P
GROUP = 8
REM = PAIRS - 4 * P
W2C = 4 * P + 96
GN_EPS = 1e-5
BN_EPS = 1e-5
GN_MAX = 182.0
TINY = 1e-30
F16_TOP = 2.0 ** 15
QK_TOP = 2.0 ** 14
M_ROWS = (2.0 ** 14, 2.0 ** 3)
LO = 2.0 ** 11
EXP_SHIFT = 8.0
SLOTS = 4
LEAD = 5

V_BQ, V_BK, V_BV, V_GAMMA, V_B1, V_G1, V_BE1, V_M1, V_V1 = 0, 1, 2, 4, 5, 6, 7, 8, 9
V_B2, V_G2, V_BE2, V_M2, V_V2, V_FROW, V_N = 10, 12, 14, 16, 18, 20, 21


def build(nc, x, wq, wk, wv, w1, w2, vec, ident, gmean, sel, out):
    f32, f16 = mybir.dt.float32, mybir.dt.float16
    ACT = mybir.ActivationFunctionType
    ALU = mybir.AluOpType
    AX = mybir.AxisListType.X
    ds = bass.ds
    ctx = ExitStack()
    with ctx:
        def sb(name, shape, dt):
            return ctx.enter_context(nc.sbuf_tensor(name, shape, dt))

        def sem(name):
            return ctx.enter_context(nc.semaphore(name))

        xa = sb("xa", [P, H2, HW], f32)
        xs = sb("xs", [P, H2, HW], f32)
        xh = sb("xh", [P, H2, HW], f16)
        xl = sb("xl", [P, H2, HW], f16)
        fst = sb("fst", [P, HW], f16)
        gst = sb("gst", [P, HW], f16)
        xn = sb("xn", [P, 2, H2, CH], f32)
        hth = sb("hth", [P, NT, C + 1], f16)
        htl = sb("htl", [P, NT, C], f16)
        p32 = sb("p32", [P, SLOTS, CH], f32)
        ph = sb("ph", [P, SLOTS, CH], f16)
        pl = sb("pl", [P, SLOTS, CH], f16)
        mx = sb("mx", [P, NT, NCH], f32)
        nm = sb("nm", [P, QT], f32)
        mw = sb("mw", [P, 5, QT], f32)
        r1 = sb("r1", [P, QT], f32)
        r2 = sb("r2", [P, QT], f32)
        r3 = sb("r3", [P, QT], f32)
        mrow = sb("mrow", [P, QT, P], f16)
        rinv = sb("rinv", [P, QT], f32)
        ot = sb("ot", [P, QT, C], f32)
        bst = [sb(f"bst{i}", [P, H2, NCH, 6], f32) for i in range(2)]
        bag = [sb(f"bag{i}", [P, H2, 2], f32) for i in range(2)]
        gin = [sb(f"gin{i}", [P, H2, 2], f32) for i in range(2)]
        gsb = [sb(f"gsb{i}", [P, H2, 2], f32) for i in range(2)]
        gmq = [sb(f"gmq{i}", [P, H2], f32) for i in range(2)]
        gve = [sb(f"gve{i}", [P, H2], f32) for i in range(2)]
        rstd = [sb(f"rstd{i}", [P, H2], f32) for i in range(2)]
        nbias = [sb(f"nbias{i}", [P, H2], f32) for i in range(2)]
        ht32 = htl[:].rearrange("p t c -> p (t c)").bitcast(f32)
        ht16 = htl[:].rearrange("p t c -> p (t c)")
        pb = ht32[:, 0:5 * CH].rearrange("p (g n) -> p g n", g=5)
        ybig = ht32[:, 5 * CH:7 * CH].rearrange("p (r n) -> p r n", r=2)
        yst = ht16[0:64, 14 * CH:16 * CH].rearrange("p (r n) -> p r n", r=2)
        qrest = sb("qrest", [P, CH], f16)
        qh = [pl[:, g] for g in range(4)] + [qrest[:]]
        ql = [ph[:, g] for g in range(4)]
        zt = p32[:].rearrange("p (r h) n -> p r h n", r=2)
        og = sb("og", [P, 2, H2, CH], f32)
        wqn = sb("wqn", [96, C], f32)
        wkn = sb("wkn", [96, C], f32)
        wvn = zt[:, 0, :, 0:C]
        w1n = sb("w1n", [P, C], f32)
        w2n = og[:].rearrange("p a h n -> p (a h n)")[:, 0:H2 * W2C].rearrange("p (h n) -> p h n", h=H2)
        vs = sb("vs", [P, V_N], f32)
        idn = sb("idn", [P, P], f32)
        idh = sb("idh", [P, P], f16)
        gm = sb("gm", [P, P], f32)
        ones = sb("ones", [P, P], f32)
        selh = sb("selh", [64, W2C], f16)
        wqT = sb("wqT", [P, 2, H2, 96], f16)
        wkT = sb("wkT", [P, 2, H2, 96], f16)
        wvT = sb("wvT", [P, 2, H2, C], f16)
        w1T = sb("w1T", [P, 2, H2, P], f16)
        w2T = sb("w2T", [P, 3, 4, C], f16)
        w2r = sb("w2r", [96, C], f16)
        sc = sb("sc", [P, 64], f32)
        exps = sb("exps", [P, 4], f32)
        carrier = sb("carrier", [P, 1], f32)
        spare = sb("spare", [P, 16], f32)
        bq = sb("bq", [96, 1], f32)
        bk = sb("bk", [96, 1], f32)
        esc = sb("esc", [P, 1], f32)
        vout = sb("vout", [P, H2], f32)
        gbv = sb("gbv", [P, H2], f32)
        s1a = sb("s1a", [P, 1], f32)
        t1a = sb("t1a", [P, 1], f32)
        sc2 = sb("sc2", [P, H2], f32)
        t2 = sb("t2", [P, H2], f32)

        acc = [ctx.enter_context(nc.psum_tensor(f"acc{i}", [P, CH], f32)) for i in range(QT)]
        sps = [ctx.enter_context(nc.psum_tensor(f"sps{i}", [P, CH], f32)) for i in range(2)]
        tps = [ctx.enter_context(nc.psum_tensor(f"tps{i}", [P, CH], f32)) for i in range(2)]

        w_in = sem("w_in")
        x_in = [sem(f"x_in{c}") for c in range(NCH)]
        x_next = sem("x_next")
        st_ok = sem("st_ok")
        set_dve = sem("set_dve")
        set_pool = sem("set_pool")
        set_pe = sem("set_pe")
        set_act = sem("set_act")
        gn_dve = sem("gn_dve")
        gn_in = sem("gn_in")
        gn_pe = sem("gn_pe")
        gn_var = sem("gn_var")
        gn_pow = sem("gn_pow")
        gn_ok = sem("gn_ok")
        xh_ok = sem("xh_ok")
        xn_act, xn_dve = sem("xn_act"), sem("xn_dve")
        xl_ok = sem("xl_ok")
        f_mm, g_mm, h_mm = sem("f_mm"), sem("g_mm"), sem("h_mm")
        f_hi, g_hi, h_hi = sem("f_hi"), sem("g_hi"), sem("h_hi")
        f_lo, g_lo, h_lo = sem("f_lo"), sem("g_lo"), sem("h_lo")
        t_mm = sem("t_mm")
        t_free = sem("t_free")
        nm_ok = sem("nm_ok")
        m_pool = sem("m_pool")
        m_rows = sem("m_rows")
        m_mm = sem("m_mm")
        m_ok = sem("m_ok")
        s_mm = sem("s_mm")
        ph_ok, p32_ok, pl_ok = sem("ph_ok"), sem("p32_ok"), sem("pl_ok")
        p_free = sem("p_free")
        acc_mm = sem("acc_mm")
        rinv_ok = sem("rinv_ok")
        ot_act = sem("ot_act")
        ot_dve = sem("ot_dve")
        o_mm = sem("o_mm")
        x1_ok = sem("x1_ok")
        bv_ok = sem("bv_ok")
        y_mm, y_ok, yh_ok, yl_ok = sem("y_mm"), sem("y_ok"), sem("yh_ok"), sem("yl_ok")
        sel_mm = sem("sel_mm")
        pb_ok, qh_ok, ql_ok = sem("pb_ok"), sem("qh_ok"), sem("ql_ok")
        z_mm, z_ok = sem("z_mm"), sem("z_ok")
        res_ok = sem("res_ok")
        og_free = [sem("og_free0"), sem("og_free1")]
        block = ctx.enter_context(nc.Block())

        class Steps:

            def __init__(self, eng, s, base=0):
                self.eng, self.s, self.base, self.n = eng, s, base, 0

            def __call__(self, ins):
                ins.then_inc(self.s, 1)
                self.n += 1
                self.eng.wait_ge(self.s, self.base + self.n)

        AHEAD = 3
        LAST_PIECES = [(t, NCH - 1) for t in range(QT)] + [(QT, NCH - 2), (QT, NCH - 1)]
        FIRST_LAST = (NCH - 1) * LEAD - 1
        NORM_AT = NCH - 4
        SPLITS = NT - QT + 1
        NLOADS = 9
        GN_STEPS = 6
        M_STEPS = 4

        xv = x.rearrange("b (h p) n -> b p h n", p=P)
        ov = out.rearrange("b (h p) n -> b p h n", p=P)
        R_BANK = [acc[1], acc[2], acc[3], tps[0], tps[1]]
        Y_BANK = acc[0]
        Z_BANK = sps

        (K_NQ, K_NK, K_PR, K_SUM, K_C2, K_A, K_BB, K_T, K_RS1, K_INV1, K_T1, K_YB, K_A2, K_AA, K_IA) = range(15)
        K_RV, K_RW, K_INV2, K_MX, K_U, K_W = 16, 18, 20, 22, 24, 26
        mark = {}

        def h_bank(c, k):
            return acc[2 * (c % 2) + k]

        @block.sync
        def _(sp):
            for dst, src in ((vs[:], vec), (wqn[:], wq), (wkn[:], wk), (wvn, wv), (w1n[:], w1), (w2n, w2), (idn[:], ident),
                             (gm[:], gmean), (selh[:], sel)):
                sp.dma_start(dst, src).then_inc(w_in, 16)
            for c in range(NCH):
                sp.dma_start(xa[:, :, c * CH:(c + 1) * CH], xv[0, :, :, c * CH:(c + 1) * CH]).then_inc(x_in[c], 16)

            def store(b, c):
                sp.wait_ge(res_ok, b * NCH + c + 1)
                sp.dma_start(ov[ds(b, 1), :, :, c * CH:(c + 1) * CH].rearrange("a p h n -> (a p) h n"),
                             og[:, c % 2]).then_inc(og_free[c % 2], 16)

            with sp.Fori(0, B - 1) as b:
                for c in range(NCH):
                    sp.wait_ge(x1_ok, 2 * (b * NCH + c + 1))
                    sp.dma_start(xa[:, :, c * CH:(c + 1) * CH],
                                 xv[ds(b + 1, 1), :, :, c * CH:(c + 1) * CH].rearrange("a p h n -> (a p) h n")
                                 ).then_inc(x_next, 16)
                    sp.wait_ge(x_next, 16 * (b * NCH + c + 1))
                for c in range(NCH):
                    store(b, c)
            sp.sem_inc(x_next, 16 * NCH)
            for c in range(NCH):
                store(B - 1, c)
            for par in range(2):
                sp.wait_ge(og_free[par], 16 * (B * NCH // 2 + 1))

        @block.vector
        def _(dve):
            V = nc.vector
            s = Steps(dve, set_dve)

            def col(k, n=1, p=P):
                return sc[0:p, k:k + n]

            def vc(k, n=1, p=P):
                return vs[0:p, k:k + n]

            carried = [0]

            def carry_wait():
                carried[0] = (carried[0] + 1) % 16
                V.memset(spare[:, carried[0]:carried[0] + 1], 0.0)

            counted = [0]

            def first_stats():
                c, h = divmod(counted[0], H2)
                counted[0] += 1
                if h == 0:
                    dve.wait_ge(x_in[c], 16)
                ins = V.bn_stats(bst[0][:, h, c], xa[:, h, c * CH:(c + 1) * CH])
                if counted[0] == H2 * NCH:
                    ins.then_inc(st_ok, 1)

            def s2(ins):
                ins.then_inc(set_dve, 1)
                s.n += 1
                if counted[0] < H2 * NCH:
                    first_stats()
                dve.wait_ge(set_dve, s.n)

            def magnitude(o, v, least, step=s):
                step(V.scalar_tensor_tensor(o, v, -1.0, v, ALU.mult, ALU.max))
                step(V.tensor_scalar(o, o, least, None, ALU.add))

            s(V.memset(gst[96:P, :], 0.0))
            mark["zeros"] = s.n
            dve.wait_ge(w_in, 16 * NLOADS)
            dve.wait_ge(set_pool, 1)
            s(V.tensor_scalar(col(K_W), vc(V_V1), BN_EPS, None, ALU.add))
            s(V.tensor_scalar(col(K_W + 1, 2), vc(V_V2, 2), BN_EPS, None, ALU.add))
            mark["variances"] = s.n
            s(V.tensor_copy(idh[:], idn[:]))
            s(V.tensor_reduce(col(K_NQ, 1, 96), wqn[:], AX, ALU.add, apply_absolute_value=True))
            s(V.tensor_reduce(col(K_NK, 1, 96), wkn[:], AX, ALU.add, apply_absolute_value=True))
            magnitude(col(K_U, 2, 96), vc(V_BQ, 2, 96), TINY)
            s(V.tensor_tensor(col(K_NQ, 2, 96), col(K_NQ, 2, 96), col(K_U, 2, 96), ALU.add))
            s(V.tensor_tensor(col(K_PR, 1, 96), col(K_NQ, 1, 96), col(K_NK, 1, 96), ALU.mult))
            mark["bounds"] = s.n
            dve.wait_ge(set_pe, 1)
            s(V.tensor_scalar(esc[:], tps[1][:, 0:1], GN_MAX ** 2 / QK_TOP ** 2, None, ALU.mult))
            s2(V.reciprocal(col(K_C2), esc[:]))
            s2(V.reciprocal(col(K_BB, 1, 96), col(K_NQ, 1, 96)))
            s2(V.scalar_tensor_tensor(col(K_T, 1, 96), col(K_NK, 1, 96), col(K_C2, 1, 96), col(K_BB, 1, 96),
                                     ALU.mult, ALU.mult))
            mark["ratio"] = s.n
            dve.wait_ge(set_pool, 3)
            s2(V.reciprocal(col(K_T, 1, 96), col(K_A, 1, 96)))
            s2(V.tensor_tensor(col(K_BB, 1, 96), col(K_T, 1, 96), col(K_C2, 1, 96), ALU.mult))
            s2(V.tensor_scalar(wqn[:], wqn[:], col(K_A, 1, 96), None, ALU.mult))
            s2(V.tensor_scalar(wkn[:], wkn[:], col(K_BB, 1, 96), None, ALU.mult))
            s2(V.tensor_tensor(bq[:], vc(V_BQ, 1, 96), col(K_A, 1, 96), ALU.mult))
            s2(V.tensor_tensor(bk[:], vc(V_BK, 1, 96), col(K_BB, 1, 96), ALU.mult))
            def moments(n, layer):
                g = Steps(dve, gn_dve, n * GN_STEPS)
                dve.wait_ge(st_ok, n + 1)
                carry_wait()
                for h in range(H2):
                    last = V.bn_aggr(bag[layer][:, h], bst[layer][:, h].rearrange("p c k -> p (c k)"))
                g(last)
                g(V.tensor_tensor(gmq[layer][:], bag[layer][:, :, 0], bag[layer][:, :, 0], ALU.mult))
                g(V.tensor_copy(gin[layer][:, :, 0], bag[layer][:, :, 0]))
                V.tensor_tensor(gin[layer][:, :, 1], bag[layer][:, :, 1], gmq[layer][:], ALU.add).then_inc(gn_in, 1)

            s2(V.tensor_reduce(col(K_RV, 2), wvn, AX, ALU.add, apply_absolute_value=True))
            s2(V.tensor_scalar(col(K_RV, 2), col(K_RV, 2), TINY, GN_MAX / F16_TOP, ALU.add, ALU.mult))
            s2(V.reciprocal(col(K_RW, 2), col(K_RV, 2)))
            for h in range(H2):
                s2(V.tensor_scalar(wvn[:, h], wvn[:, h], col(K_RW + h), None, ALU.mult))
            s2(V.tensor_scalar(vout[:], col(K_RV, 2), vc(V_GAMMA), None, ALU.mult))
            s2(V.tensor_scalar(gbv[:], vc(V_BV, 2), vc(V_GAMMA), None, ALU.mult))
            s2(V.tensor_scalar(mw[:, 4], mw[:, 0], 0.0, col(K_C2), ALU.mult, ALU.add))
            s2(V.tensor_scalar(mw[:, 4], mw[:, 4], EXP_SHIFT, None, ALU.mult))
            mark["scaled_qkv"] = s.n
            s2(V.tensor_reduce(col(K_MX, 2), w2n, AX, ALU.max, apply_absolute_value=True))
            s2(V.tensor_scalar(col(K_MX, 2), col(K_MX, 2), TINY, 2.0 ** -14, ALU.add, ALU.mult))
            s2(V.reciprocal(col(K_U, 2), col(K_MX, 2)))
            for h in range(H2):
                s2(V.tensor_scalar(w2n[:, h], w2n[:, h], col(K_U + h), None, ALU.mult))
            s2(V.tensor_reduce(col(K_RS1), w1n[:], AX, ALU.add, apply_absolute_value=True))
            s2(V.tensor_tensor(col(K_INV1), vc(V_G1), col(K_W), ALU.mult))
            s2(V.tensor_tensor(col(K_YB), col(K_RS1), col(K_INV1), ALU.mult))
            s2(V.tensor_scalar(col(K_RS1), col(K_RS1), TINY, 2.0 ** -7, ALU.add, ALU.mult))
            s2(V.reciprocal(col(K_U), col(K_RS1)))
            s2(V.tensor_scalar(w1n[:], w1n[:], col(K_U), None, ALU.mult))
            mark["scaled"] = s.n
            s2(V.tensor_tensor(col(K_T1), vc(V_B1), vc(V_M1), ALU.subtract))
            s2(V.scalar_tensor_tensor(col(K_T1), col(K_T1), col(K_INV1), vc(V_BE1), ALU.mult, ALU.add))
            magnitude(col(K_T), col(K_YB), 0.0, s2)
            s2(V.tensor_scalar(col(K_YB), col(K_T), GN_MAX, None, ALU.mult))
            magnitude(col(K_U), col(K_T1), 1e-15, s2)
            s2(V.tensor_tensor(col(K_YB), col(K_YB), col(K_U), ALU.add))
            s2(V.tensor_tensor(col(K_YB), col(K_YB), col(K_YB), ALU.mult))
            mark["squares"] = s.n
            dve.wait_ge(set_act, 1)
            V.tensor_tensor(wqT[:, 1], acc[0][:, 0:192].rearrange("p (h c) -> p h c", h=2), wqT[:, 0], ALU.subtract)
            V.tensor_tensor(wkT[:, 1], acc[1][:, 0:192].rearrange("p (h c) -> p h c", h=2), wkT[:, 0], ALU.subtract)
            s2(V.tensor_tensor(wvT[:, 1], acc[2][:].rearrange("p (h c) -> p h c", h=2), wvT[:, 0], ALU.subtract))
            mark["weights_qkv"] = s.n
            while counted[0] < H2 * NCH:
                first_stats()
            moments(0, 0)
            dve.wait_ge(set_pe, 4)
            s2(V.tensor_scalar(col(K_T), tps[1][:, 8:9], 1.0 / F16_TOP, None, ALU.mult))
            s2(V.reciprocal(col(K_A2), col(K_T)))
            mark["square"] = s.n
            s2(V.tensor_tensor(col(K_INV2, 2), vc(V_G2, 2), col(K_W + 1, 2), ALU.mult))
            s2(V.tensor_tensor(t2[:], vc(V_B2, 2), vc(V_M2, 2), ALU.subtract))
            s2(V.tensor_tensor(t2[:], t2[:], col(K_INV2, 2), ALU.mult))
            s2(V.tensor_tensor(t2[:], t2[:], vc(V_BE2, 2), ALU.add))
            s2(V.tensor_tensor(col(K_INV2, 2), col(K_INV2, 2), col(K_MX, 2), ALU.mult))

            def variance(n, layer):
                g = Steps(dve, gn_dve, n * GN_STEPS + 3)
                gs, gq, gv = gsb[layer], gmq[layer], gve[layer]
                dve.wait_ge(gn_pe, n + 1)
                g(V.tensor_copy(gs[:].rearrange("p h k -> p (h k)"), Y_BANK[:, 0:4]))
                g(V.tensor_tensor(gq[:], gs[:, :, 0], gs[:, :, 0], ALU.mult))
                g(V.tensor_tensor(gv[:], gs[:, :, 1], gq[:], ALU.subtract))
                V.tensor_scalar(gv[:], gv[:], 0.0, GN_EPS, ALU.max, ALU.add).then_inc(gn_var, 1)

            def bias(n, layer):
                dve.wait_ge(gn_pow, n + 1)
                V.scalar_tensor_tensor(nbias[layer][:], gsb[layer][:, :, 0], -1.0, rstd[layer][:], ALU.mult,
                                       ALU.mult).then_inc(gn_ok, 1)

            def normed(b, c):
                at = slice(c * CH, (c + 1) * CH)
                dve.wait_ge(xl_ok, (b * 2 + 1) * NCH + c + 1)
                for h in range(H2 if c < AHEAD else 1):
                    last = V.tensor_scalar(xn[:, c % 2, h], xs[:, h, at], rstd[1][:, h:h + 1], nbias[1][:, h:h + 1],
                                           ALU.mult, ALU.add)
                last.then_inc(xn_dve, 1)

            def first_low(b, layer):
                dve.wait_ge(xh_ok, b * (2 * NCH) + layer * NCH + 1)
                for h in range(H2):
                    last = V.tensor_tensor(xl[:, h, 0:CH], xn[:, 0, h], xh[:, h, 0:CH], ALU.subtract)
                last.then_inc(xl_ok, 1)

            def query_low(n, c):
                at = slice(c * CH, (c + 1) * CH)
                dve.wait_ge(f_hi, n + 1)
                V.scalar_tensor_tensor(fst[64:96, at], sps[0][64:96, :], bq[64:96], fst[64:96, at],
                                       ALU.add, ALU.subtract).then_inc(f_lo, 1)

            def key_low(n, c):
                at = slice(c * CH, (c + 1) * CH)
                dve.wait_ge(g_hi, n + 1)
                V.scalar_tensor_tensor(gst[32:64, at], sps[1][32:64, :], bk[32:64], gst[32:64, at],
                                       ALU.add, ALU.subtract).then_inc(g_lo, 1)

            def value_low(n, c, k):
                dve.wait_ge(h_hi, 2 * n + k + 1)
                t = c * QT + 2 * k
                V.tensor_tensor(htl[:, t:t + 2], h_bank(c, k)[:].rearrange("p (t c) -> p t c", t=2),
                                hth[:, t:t + 2, 0:C], ALU.subtract).then_inc(h_lo, 1)

            def piece_max(n, tile, c, par):
                dve.wait_ge(t_mm, n + 1)
                V.reduce_max(mx[:, ds(tile, 1), c], tps[par][:], AX).then_inc(t_free, 1)

            def tile_max(n, tile, k):
                dve.wait_ge(t_free, n + 2)
                carry_wait()
                V.tensor_reduce(nm[:, k:k + 1], mx[:, ds(tile, 1)], AX, ALU.max, negate=True).then_inc(nm_ok, 1)

            def finish_block(n, J, half_):
                dve.wait_ge(o_mm, 2 * n + half_ + 1)
                at = ds(J * CH, CH)
                V.scalar_tensor_tensor(xs[:, half_, at], tps[1 - half_][:], vout[:, half_:half_ + 1],
                                       xa[:, half_, at], ALU.mult, ALU.add).then_inc(x1_ok, 1)

            def stats(n, J, half_):
                dve.wait_ge(x1_ok, 2 * n + half_ + 1)
                return V.bn_stats(bst[1][:, half_, ds(J, 1)].rearrange("p a k -> p (a k)"), xs[:, half_, ds(J * CH, CH)])

            def next_stats(b, c, h):
                dve.wait_ge(x_next, 16 * (b * NCH + c + 1))
                return V.bn_stats(bst[0][:, h, ds(c, 1)].rearrange("p a k -> p (a k)"), xa[:, h, ds(c * CH, CH)])

            def divide(b, J):
                n = b * NCH + J
                for j in range(QT):
                    if j + 1 < QT:
                        dve.wait_ge(acc_mm, n * (QT - 1) + j + 1)
                    else:
                        dve.wait_ge(p_free, SLOTS + (n + 1) * NT)
                    V.reciprocal(rinv[:, j:j + 1], acc[j][:, C:C + 1]).then_inc(rinv_ok, 1)
                for j in (2, 3):
                    dve.wait_ge(rinv_ok, n * QT + j + 1)
                    V.tensor_scalar(ot[:, j], acc[j][:, 0:C], rinv[:, j:j + 1], None, ALU.mult).then_inc(ot_dve, 1)

            def group(b, J, q, maxima=True, pending=True, finish=False, closing=False):
                k = J * QT + q
                T = b * (NT * NCH) + J * NT + q * 8
                N = b * (NT * NCH) + (k + LEAD) * 8
                for u in range(8):
                    dve.wait_ge(p32_ok, T + u + 1)
                    V.tensor_tensor(pl[:, u % SLOTS], p32[:, u % SLOTS], ph[:, u % SLOTS],
                                    ALU.subtract).then_inc(pl_ok, 1)
                    if closing and u == 7:
                        divide(b, J)
                    if u == 0 and pending:
                        piece_max(N - 1, k + LEAD - 1, 7, 1)
                        tile_max(N, k + LEAD - 1, (q + LEAD - 1) % QT)
                    if finish and u in (1, 2):
                        if u == 1:
                            dve.wait_ge(bv_ok, b + 1)
                        finish_block(b * NCH + J - 1, J - 1, u - 1)
                    if finish and u in (2, 3):
                        stats(b * NCH + J - 1, J - 1, u - 2)
                    if finish and u in (6, 7):
                        next_stats(b, J - 1, u - 6)
                    if maxima and u:
                        piece_max(N + u - 1, k + LEAD, u - 1, (u - 1) % 2)

            def products(n, g, par):
                rows = P if g < 4 else 96
                dve.wait_ge(sel_mm, 5 * n + g + 1)
                dve.wait_ge(y_ok, n + 1)
                V.tensor_tensor(pb[0:rows, g], ybig[0:rows, par], R_BANK[g][0:rows, :],
                                ALU.mult).then_inc(pb_ok, 1)

            def product_low(n, g):
                dve.wait_ge(qh_ok, 5 * n + g + 1)
                if g < 4:
                    V.scalar_tensor_tensor(ql[g], qh[g], -LO, pb[:, g], ALU.mult,
                                           ALU.add).then_inc(ql_ok, 1)
                else:
                    V.scalar_tensor_tensor(qh[g][64:96, :], qh[g][64:96, :], -LO, pb[64:96, g], ALU.mult,
                                           ALU.add).then_inc(ql_ok, 1)

            def y_low(n, par):
                dve.wait_ge(yh_ok, n + 1)
                V.scalar_tensor_tensor(yst[32:64, par], yst[32:64, par], -LO, ybig[32:64, par], ALU.mult,
                                       ALU.add).then_inc(yl_ok, 1)

            variance(0, 0)
            dve.wait_ge(set_act, 2)
            V.tensor_tensor(w1T[:, 1], acc[3][:, 0:256].rearrange("p (h c) -> p h c", h=2), w1T[:, 0], ALU.subtract)
            V.tensor_tensor(w2T[:, 1, 0:2], sps[0][:].rearrange("p (g c) -> p g c", g=2), w2T[:, 0, 0:2], ALU.subtract)
            V.tensor_tensor(w2T[:, 1, 2:4], sps[1][:].rearrange("p (g c) -> p g c", g=2), w2T[:, 0, 2:4], ALU.subtract)
            s(V.tensor_tensor(w2r[32:64, :], tps[0][32:64, 0:C], w2r[32:64, :], ALU.subtract))
            mark["weights"] = s.n
            bias(0, 0)
            dve.wait_ge(gn_ok, 1)
            for h in range(H2):
                last = V.tensor_scalar(xn[:, 0, h], xa[:, h, 0:CH], rstd[0][:, h:h + 1], nbias[0][:, h:h + 1],
                                       ALU.mult, ALU.add)
            s(last)
            first_low(0, 0)
            dve.wait_ge(set_pool, 4)
            s(V.tensor_tensor(col(K_T), col(K_AA), col(K_AA), ALU.mult))
            s(V.reciprocal(col(K_IA), col(K_T)))
            s(V.tensor_scalar(sc2[:], col(K_INV2, 2), col(K_IA), None, ALU.mult))
            s(V.tensor_scalar(col(K_AA), col(K_AA), LO, None, ALU.mult))
            s(V.tensor_tensor(col(K_T), col(K_INV1), col(K_RS1), ALU.mult))
            s(V.tensor_tensor(s1a[:], col(K_T), col(K_AA), ALU.mult))
            s(V.tensor_tensor(t1a[:], col(K_T1), col(K_AA), ALU.mult))
            with dve.Fori(0, B) as b:
                for c in range(NCH):
                    n = b * NCH + c

                    def early(t, c=c):
                        if c and t < LEAD:
                            i = (c - 1) * LEAD + t
                            piece_max(b * (NT * NCH) + i, t, c - 1, i % 2)

                    early(0)
                    query_low(n, c)
                    early(1)
                    key_low(n, c)
                    if c < NCH - 1:
                        value_low(n, c, 0)
                    early(2)
                    if c < NCH - 1:
                        value_low(n, c, 1)
                    early(3)
                    if c < NCH - 1:
                        early(4)
                for i, (t, c) in enumerate(LAST_PIECES):
                    i += FIRST_LAST
                    piece_max(b * (NT * NCH) + i, t, c, i % 2)
                    if (t, c) == (QT - 1, NCH - 1):
                        dve.wait_ge(t_free, b * (NT * NCH) + i + 1 + 2)
                        carry_wait()
                        V.tensor_reduce(nm[:, 0:QT], mx[:, 0:QT], AX, ALU.max, negate=True).then_inc(nm_ok, QT)
                        value_low(b * NCH + NCH - 1, NCH - 1, 0)
                        value_low(b * NCH + NCH - 1, NCH - 1, 1)
                for t in range(QT, LEAD):
                    dve.wait_ge(m_rows, b * NT + t - QT + 1)
                    tile_max(b * (NT * NCH) + NCH * LEAD, t, t % QT)
                group(b, 0, 0, pending=False)
                with dve.Fori(0, NCH - 2) as J:
                    for q in (1, 2, 3):
                        group(b, J, q, closing=(q == 3))
                    group(b, J + 1, 0, finish=True)
                for q in (1, 2, 3):
                    group(b, NCH - 2, q, maxima=(q < 3), closing=(q == 3))
                group(b, NCH - 1, 0, maxima=False, pending=False, finish=True)
                for q in (1, 2, 3):
                    group(b, NCH - 1, q, maxima=False, pending=False, closing=(q == 3))
                for h in range(H2):
                    finish_block(b * NCH + NCH - 1, NCH - 1, h)
                for h in range(H2):
                    last = stats(b * NCH + NCH - 1, NCH - 1, h)
                last.then_inc(st_ok, 1)
                moments(b * 2 + 1, 1)
                variance(b * 2 + 1, 1)
                bias(b * 2 + 1, 1)
                dve.wait_ge(gn_ok, b * 2 + 2)
                normed(b, 0)
                dve.wait_ge(xn_dve, b * NCH + 1)
                first_low(b, 1)
                for c in range(1, AHEAD):
                    normed(b, c)
                y_low(b * NCH, 0)
                products(b * NCH, 0, 0)
                products(b * NCH, 1, 0)
                for c in range(NCH):
                    n = b * NCH + c
                    more = c + 1 < NCH
                    product_low(n, 0)
                    products(n, 2, c % 2)
                    product_low(n, 1)
                    products(n, 3, c % 2)
                    if more:
                        y_low(n + 1, (c + 1) % 2)
                    product_low(n, 2)
                    products(n, 4, c % 2)
                    if c == NORM_AT + 1:
                        bias(b * 2 + 2, 0)
                    product_low(n, 3)
                    if more:
                        products(n + 1, 0, (c + 1) % 2)
                    product_low(n, 4)
                    if more:
                        products(n + 1, 1, (c + 1) % 2)
                    if c + AHEAD < NCH:
                        normed(b, c + AHEAD)
                    if c == 0:
                        for h in range(H2):
                            last = next_stats(b, NCH - 1, h)
                        last.then_inc(st_ok, 1)
                    if c == 1:
                        moments(b * 2 + 2, 0)
                    if c == NORM_AT:
                        variance(b * 2 + 2, 0)

        @block.gpsimd
        def _(pool):
            nc.gpsimd.memset(exps[:, 0:3], -0.5).then_inc(xl_ok, 2)
            nc.gpsimd.memset(exps[:, 3:4], 0.5).then_inc(t_free, 2)
            nc.gpsimd.memset(mrow[:, 0:1], 0.0).then_inc(p_free, SLOTS)
            nc.gpsimd.memset(mrow[:, 1:2], 0.0).then_inc(ot_act, 2)
            nc.gpsimd.memset(ones[:, 0:P // 4], 1.0).then_inc(ot_dve, 2)
            nc.gpsimd.memset(mrow[:, 2:QT], 0.0).then_inc(m_ok, QT)
            nc.gpsimd.memset(hth[:, :, C:C + 1], 1.0).then_inc(og_free[0], 16)
            nc.gpsimd.memset(ones[:, P // 4:P // 2], 1.0).then_inc(og_free[1], 16)
            nc.gpsimd.memset(carrier[:], 0.0).then_inc(xn_act, 1)
            for i in range(2):
                nc.gpsimd.memset(mw[:, i], M_ROWS[i])
                nc.gpsimd.memset(mw[:, 2 + i], 1 / M_ROWS[i])
            nc.gpsimd.memset(ones[:, P // 2:], 1.0).then_inc(set_pool, 1)
            pool.wait_ge(set_pool, 1)
            pool.wait_ge(set_dve, mark["variances"])
            nc.gpsimd.tensor_tensor(sc[:, K_W:K_W + 3], sc[:, K_W:K_W + 3], exps[:, 0:3],
                                    ALU.pow).then_inc(set_pool, 1)
            pool.wait_ge(set_dve, mark["ratio"])
            nc.gpsimd.tensor_tensor(sc[0:96, K_A:K_A + 1], sc[0:96, K_T:K_T + 1], exps[0:96, 3:4],
                                    ALU.pow).then_inc(set_pool, 1)
            pool.wait_ge(set_dve, mark["square"])
            nc.gpsimd.tensor_tensor(sc[:, K_AA:K_AA + 1], sc[:, K_A2:K_A2 + 1], exps[:, 3:4],
                                    ALU.pow).then_inc(set_pool, 1)

            def power(n, layer):
                pool.wait_ge(gn_var, n)
                nc.gpsimd.tensor_tensor(rstd[layer][:], gve[layer][:], exps[:, 0:2], ALU.pow).then_inc(gn_pow, 1)

            def low(b, layer, c):
                at = slice(c * CH, (c + 1) * CH)
                pool.wait_ge(xh_ok, (b * 2 + layer) * NCH + c + 1)
                pool.wait_ge(xn_dve if layer else xn_act, b * NCH + c + 1)
                for h in range(H2):
                    last = nc.gpsimd.tensor_tensor(xl[:, h, at], xn[:, c % 2, h], xh[:, h, at], ALU.subtract)
                last.then_inc(xl_ok, 1)

            def split_max(n, k, splits):
                pool.wait_ge(nm_ok, n + 1)
                pool.wait_ge(m_ok, n + 1)
                wide = k.stop - k.start
                step = Steps(pool, m_pool, splits * M_STEPS)
                tt = nc.gpsimd.tensor_tensor

                def wt(i):
                    return mw[:, i, 0:wide]

                step(tt(r3[:, k], nm[:, k], wt(4), ALU.add))
                step(tt(mrow[:, k, 96], r3[:, k], wt(2), ALU.mult))
                step(tt(r2[:, k], mrow[:, k, 96], wt(0), ALU.mult))
                step(tt(r1[:, k], r3[:, k], r2[:, k], ALU.subtract))
                tt(mrow[:, k, 97], r1[:, k], wt(3), ALU.mult).then_inc(m_rows, wide)

            def residual(b, c):
                pool.wait_ge(z_ok, 2 * (b * NCH + c + 1))
                pool.wait_ge(og_free[c % 2], 16 * (b * (NCH // 2) + c // 2 + 1))
                for h in range(H2):
                    last = nc.gpsimd.tensor_tensor(og[:, c % 2, h], xs[:, h, c * CH:(c + 1) * CH],
                                                   zt[:, c % 2, h], ALU.add)
                last.then_inc(res_ok, 1)

            power(1, 0)
            pool.wait_ge(xl_ok, 3)
            for c in range(1, AHEAD):
                low(0, 0, c)
            with pool.Fori(0, B) as b:
                for c in range(AHEAD, NCH):
                    low(b, 0, c)
                pool.wait_ge(xh_ok, b * (2 * NCH) + NCH)
                pool.wait_ge(xn_act, b * NCH + NCH)
                nc.gpsimd.tensor_tensor(carrier[:], exps[:, 0:1], exps[:, 0:1], ALU.mult)
                for h in range(H2):
                    last = nc.gpsimd.tensor_scalar(xa[:, h], xa[:, h], 1.0, gbv[:, h:h + 1], ALU.mult, ALU.add)
                last.then_inc(bv_ok, 1)
                split_max(b * NT + QT - 1, slice(0, QT), b * SPLITS)
                with pool.Fori(1, NT // QT) as jj:
                    for u in range(QT):
                        split_max(b * NT + jj * QT + u, slice(u, u + 1), b * SPLITS + 1 - QT + jj * QT + u)
                power(b * 2 + 2, 1)
                pool.wait_ge(xl_ok, b * (2 * NCH) + NCH + 3)
                for c in range(1, AHEAD):
                    low(b, 1, c)
                for c in range(NCH):
                    if c + AHEAD < NCH:
                        low(b, 1, c + AHEAD)
                    if c == NORM_AT:
                        power(b * 2 + 3, 0)
                    if c == NORM_AT + 1:
                        low(b + 1, 0, 0)
                    if c == NORM_AT + 2:
                        low(b + 1, 0, 1)
                    residual(b, c)
                low(b + 1, 0, 2)

        @block.scalar
        def _(act):
            A = nc.scalar.activation
            act.wait_ge(set_pool, 1)
            act.wait_ge(set_dve, mark["zeros"])
            act.wait_ge(w_in, 16 * NLOADS)
            A(fst[96:P, :], gst[96:P, :], ACT.Identity, bias=vs[96:P, V_FROW:V_FROW + 1])
            act.wait_ge(set_pe, 2)
            A(wqT[:, 0], acc[0][:, 0:192].rearrange("p (h c) -> p h c", h=2), ACT.Copy)
            A(wkT[:, 0], acc[1][:, 0:192].rearrange("p (h c) -> p h c", h=2), ACT.Copy)
            A(wvT[:, 0], acc[2][:].rearrange("p (h c) -> p h c", h=2), ACT.Copy).then_inc(set_act, 1)
            act.wait_ge(set_pe, 3)
            A(w1T[:, 0], acc[3][:, 0:256].rearrange("p (h c) -> p h c", h=2), ACT.Copy)
            A(w2T[:, 0, 0:2], sps[0][:].rearrange("p (g c) -> p g c", g=2), ACT.Copy)
            A(w2T[:, 0, 2:4], sps[1][:].rearrange("p (g c) -> p g c", g=2), ACT.Copy)
            A(w2r[:], tps[0][0:96, 0:C], ACT.Copy).then_inc(set_act, 1)
            act.wait_ge(set_act, 2)
            A(w2T[:, 2], w2T[:, 0], ACT.Copy, scale=1.0 / LO)
            A(w2r[64:96, :], w2r[64:96, :], ACT.Copy, scale=1.0 / LO).then_inc(set_act, 1)

            def high(b, layer, c, h):
                last = A(xh[:, h, c * CH:(c + 1) * CH], (xs if layer else xa)[:, h, c * CH:(c + 1) * CH],
                         ACT.Identity, bias=nbias[layer][:, h:h + 1], scale=rstd[layer][:, h:h + 1])
                if h == H2 - 1:
                    last.then_inc(xh_ok, 1)

            def normed(b, c, h):
                if h == 0:
                    act.wait_ge(xl_ok, b * (2 * NCH) + c + 1)
                last = A(xn[:, c % 2, h], xa[:, h, c * CH:(c + 1) * CH], ACT.Identity,
                         bias=nbias[0][:, h:h + 1], scale=rstd[0][:, h:h + 1])
                if h == H2 - 1:
                    last.then_inc(xn_act, 1)

            def norm(b, c):
                for h in range(H2):
                    high(b, 0, c, h)
                for h in range(H2):
                    normed(b, c, h)

            def project_high(n, c):
                at = slice(c * CH, (c + 1) * CH)
                act.wait_ge(f_mm, n + 1)
                A(fst[0:96, at], sps[0][0:96, :], ACT.Identity, bias=bq[:]).then_inc(f_hi, 1)
                act.wait_ge(g_mm, n + 1)
                A(gst[0:96, at], sps[1][0:96, :], ACT.Identity, bias=bk[:]).then_inc(g_hi, 1)
                for k in range(2):
                    act.wait_ge(h_mm, 2 * n + k + 1)
                    t = c * QT + 2 * k
                    A(hth[:, t:t + 2, 0:C], h_bank(c, k)[:].rearrange("p (t c) -> p t c", t=2),
                      ACT.Copy).then_inc(h_hi, 1)

            def divide(b, J):
                for j in (0, 1):
                    act.wait_ge(rinv_ok, (b * NCH + J) * QT + j + 1)
                    A(ot[:, j], acc[j][:, 0:C], ACT.Copy, scale=rinv[:, j:j + 1]).then_inc(ot_act, 1)

            def group(b, J, q, rows=True, finish=False):
                k = J * QT + q
                T = b * (NT * NCH) + J * NT + q * 8
                for u in range(8):
                    act.wait_ge(s_mm, T + u + 1)
                    act.wait_ge(p_free, T + u + 1)
                    A(ph[:, u % SLOTS], sps[u % 2][:], ACT.Exp, scale=esc[:]).then_inc(ph_ok, 1)
                    A(p32[:, u % SLOTS], sps[u % 2][:], ACT.Exp, scale=esc[:]).then_inc(p32_ok, 1)
                    if finish and u == 1:
                        divide(b, J - 1)
                    if rows and u == 4:
                        act.wait_ge(m_mm, b * NT + k + LEAD)
                        A(gst[96:98, ds((k + LEAD - 1) * P, P)], tps[0][96:98, 0:P], ACT.Copy).then_inc(m_ok, 1)

            def y_out(n, par):
                act.wait_ge(y_mm, n + 1)
                A(ybig[:, par], Y_BANK[:], ACT.Relu, bias=t1a[:], scale=s1a[:]).then_inc(y_ok, 1)

            def y_high(n, par):
                act.wait_ge(y_ok, n + 1)
                A(yst[:, par], ybig[0:64, par], ACT.Copy, scale=1.0 / LO).then_inc(yh_ok, 1)

            def z_out(n, c):
                for h in range(H2):
                    act.wait_ge(z_mm, 2 * n + h + 1)
                    if c >= 2:
                        act.wait_ge(res_ok, n - 1)
                    A(zt[:, c % 2, h], Z_BANK[h][:], ACT.Relu, bias=t2[:, h:h + 1],
                      scale=sc2[:, h:h + 1]).then_inc(z_ok, 1)

            def product_high(n, g):
                rows = P if g < 4 else 96
                act.wait_ge(pb_ok, 5 * n + g + 1)
                A(qh[g][0:rows, :], pb[0:rows, g], ACT.Copy, scale=1.0 / LO).then_inc(qh_ok, 1)

            act.wait_ge(gn_ok, 1)
            for h in range(H2):
                high(0, 0, 0, h)
            for c in range(1, AHEAD):
                norm(0, c)
            with act.Fori(0, B) as b:
                for c in range(NCH):
                    if c + AHEAD < NCH:
                        norm(b, c + AHEAD)
                    project_high(b * NCH + c, c)
                act.wait_ge(m_mm, b * NT + QT)
                A(gst[96:98, 0:CH], tps[0][96:98, :], ACT.Copy).then_inc(m_ok, QT)
                group(b, 0, 0)
                with act.Fori(0, NCH - 2) as J:
                    for q in (1, 2, 3):
                        group(b, J, q)
                    group(b, J + 1, 0, finish=True)
                for q in (1, 2, 3):
                    group(b, NCH - 2, q)
                group(b, NCH - 1, 0, rows=False, finish=True)
                for q in (1, 2, 3):
                    group(b, NCH - 1, q, rows=False)
                divide(b, NCH - 1)
                act.wait_ge(gn_ok, 2 * b + 2)
                for c in range(AHEAD - 1):
                    for h in range(H2):
                        high(b, 1, c, h)
                y_out(b * NCH, 0)
                y_high(b * NCH, 0)
                for h in range(H2):
                    high(b, 1, AHEAD - 1, h)
                product_high(b * NCH, 0)
                for c in range(NCH):
                    n = b * NCH + c
                    more = c + 1 < NCH
                    if c:
                        z_out(n - 1, c - 1)
                    if more:
                        y_out(n + 1, (c + 1) % 2)
                    product_high(n, 1)
                    if more:
                        y_high(n + 1, (c + 1) % 2)
                    product_high(n, 2)
                    if c + AHEAD < NCH:
                        act.wait_ge(xl_ok, (b * 2 + 1) * NCH + c + AHEAD + 1)
                        A(xn[:, (c + AHEAD) % 2, 1], xs[:, 1, (c + AHEAD) * CH:(c + AHEAD + 1) * CH], ACT.Identity,
                          bias=nbias[1][:, 1:2], scale=rstd[1][:, 1:2])
                        high(b, 1, c + AHEAD, 0)
                    if c == NORM_AT + 1:
                        act.wait_ge(gn_ok, 2 * b + 3)
                        high(b + 1, 0, 0, 0)
                        high(b + 1, 0, 0, 1)
                    if c == NORM_AT + 2:
                        high(b + 1, 0, 1, 0)
                        high(b + 1, 0, 1, 1)
                    product_high(n, 3)
                    if c + AHEAD < NCH:
                        high(b, 1, c + AHEAD, 1)
                    if c in (NORM_AT + 1, NORM_AT + 2):
                        normed(b + 1, c - NORM_AT - 1, 0)
                        normed(b + 1, c - NORM_AT - 1, 1)
                    product_high(n, 4)
                    if more:
                        product_high(n + 1, 0)
                z_out(b * NCH + NCH - 1, NCH - 1)
                norm(b + 1, 2)

        @block.tensor
        def _(pe):
            mm = nc.tensor.matmul
            pe.wait_ge(w_in, 16 * NLOADS)
            pe.wait_ge(set_pool, 1)
            pe.wait_ge(set_dve, mark["bounds"])
            mm(tps[1][:, 0:1], ones[0:CK, :], sc[0:CK, K_PR:K_PR + 1], start=True, stop=True).then_inc(set_pe, 1)
            tr = nc.tensor.transpose
            pe.wait_ge(set_dve, mark["scaled_qkv"])
            for i in range(H2):
                at = slice(i * P, (i + 1) * P)
                tr(acc[0][:, i * 96:(i + 1) * 96], wqn[:, at], idn[0:96, 0:96])
                tr(acc[1][:, i * 96:(i + 1) * 96], wkn[:, at], idn[0:96, 0:96])
                for o in range(H2):
                    last = tr(acc[2][:, i * C + o * P:i * C + (o + 1) * P], wvn[:, o, at], idn[:])
            last.then_inc(set_pe, 1)
            pe.wait_ge(set_dve, mark["scaled"])
            for i in range(H2):
                at = slice(i * P, (i + 1) * P)
                tr(acc[3][:, at], w1n[:, at], idn[:])
                for g in range(4):
                    tr(sps[g // 2][:, (g % 2) * C + i * P:(g % 2) * C + (i + 1) * P],
                       w2n[:, i, g * P:(g + 1) * P], idn[:])
                last = tr(tps[0][0:96, i * P:(i + 1) * P], w2n[:, i, 4 * P:W2C], idn[:])
            last.then_inc(set_pe, 1)
            pe.wait_ge(set_dve, mark["squares"])
            mm(tps[1][:, 8:9], ones[0:MID, :], sc[0:MID, K_YB:K_YB + 1], start=True, stop=True).then_inc(set_pe, 1)
            pe.wait_ge(set_dve, mark["weights_qkv"])

            def three(out, wT, at, cols):
                for i in range(H2):
                    for w, v in ((0, xh), (0, xl), (1, xh)):
                        last = mm(out, wT[:, w, i, cols], v[:, i, at], start=(i == 0 and w == 0 and v is xh),
                                  stop=(i == H2 - 1 and w == 1))
                return last

            def moments(n, layer):
                pe.wait_ge(gn_in, n + 1)
                mm(Y_BANK[:, 0:4], gm[:], gin[layer][:].rearrange("p h k -> p (h k)"), start=True,
                   stop=True).then_inc(gn_pe, 1)

            def queries(b, c):
                n = b * NCH + c
                pe.wait_ge(xl_ok, b * (2 * NCH) + c + 3)
                if c:
                    pe.wait_ge(f_lo, n)
                three(sps[0][0:96, :], wqT, slice(c * CH, (c + 1) * CH), slice(0, 96)).then_inc(f_mm, 1)

            def keys(b, c):
                n = b * NCH + c
                if c:
                    pe.wait_ge(g_lo, n)
                three(sps[1][0:96, :], wkT, slice(c * CH, (c + 1) * CH), slice(0, 96)).then_inc(g_mm, 1)

            def values(b, c, k):
                n = b * NCH + c
                if c >= 2:
                    pe.wait_ge(h_lo, 2 * (n - 2) + k + 1)
                for e in range(2):
                    t = (c * QT + 2 * k + e) * P
                    for i in range(H2):
                        for w, v in ((0, xh), (1, xh), (0, xl)):
                            last = mm(h_bank(c, k)[:, e * C:(e + 1) * C], v[:, i, t:t + P], wvT[:, w, i],
                                      start=(i == 0 and w == 0 and v is xh), stop=(i == H2 - 1 and v is xl))
                last.then_inc(h_mm, 1)

            def piece(n, tile, c, par):
                pe.wait_ge(t_free, n + 1)
                mm(tps[par][:], gst[0:96, ds(tile * P, P)], fst[0:96, c * CH:(c + 1) * CH], start=True,
                   stop=True).then_inc(t_mm, 1)

            def scores(T, tile, J, par, first=False):
                if not first:
                    pe.wait_ge(p32_ok, T - 1)
                mm(sps[par][:], fst[:, tile * P:(tile + 1) * P], gst[:, ds(J * CH, CH)], start=True,
                   stop=True).then_inc(s_mm, 1)

            def transposed(n, h):
                pe.wait_ge(ot_act, 2 * (n + 2))
                pe.wait_ge(ot_dve, 2 * (n + 2))
                for j in range(QT):
                    last = tr(tps[1 - h][:, j * P:(j + 1) * P], ot[:, j, h * P:(h + 1) * P], idn[:])
                last.then_inc(o_mm, 1)

            def group(b, J, q, maxima=True, rows=True, finish=False, end=False):
                k = J * QT + q
                T = b * (NT * NCH) + J * NT + q * 8
                N = b * (NT * NCH) + (k + LEAD) * 8
                for u in range(8):
                    t = q * 8 + u
                    if t + 2 < NT:
                        scores(T + u + 2, t + 2, J, u % 2)
                    elif not end:
                        if t + 2 == NT:
                            pe.wait_ge(m_ok, b * NT + (J + 2) * QT + QT)
                        scores(T + u + 2, t + 2 - NT, J + 1, u % 2)
                    if rows and u == 4:
                        tile = k + LEAD - 1
                        if maxima:
                            pe.wait_ge(t_free, N + u + 1)
                        pe.wait_ge(m_rows, b * NT + tile + 1)
                        mm(tps[0][:, 0:P], mrow[:, (q + LEAD - 1) % QT], idh[:], start=True,
                           stop=True).then_inc(m_mm, 1)
                    if finish and u in (1, 2):
                        n = b * NCH + J - 1
                        if maxima:
                            pe.wait_ge(t_free, N + u + 1)
                        transposed(n, u - 1)
                    slot = u % SLOTS
                    pe.wait_ge(ph_ok, T + u + 1)
                    for j in range(QT):
                        if t == 0:
                            pe.wait_ge(ot_act if j < 2 else ot_dve, (b * NCH + J) * 2 + j % 2 + 1)
                        w = ph[:, slot, j * P:(j + 1) * P]
                        mm(acc[j][:, 0:C + 1], w, hth[:, t], start=(t == 0), stop=False)
                        mm(acc[j][:, 0:C], w, htl[:, t], start=False, stop=False)
                    if rows and u == 4:
                        pe.wait_ge(m_ok, b * NT + tile + 1 + QT)
                    if finish and u in (1, 2):
                        pe.wait_ge(x1_ok, 2 * n + u)
                    if maxima:
                        piece(N + u, k + LEAD, u, u % 2)
                    pe.wait_ge(pl_ok, T + u + 1)
                    for j in range(QT):
                        last = mm(acc[j][:, 0:C + 1], pl[:, slot, j * P:(j + 1) * P], hth[:, t], start=False,
                                  stop=(t == NT - 1))
                        if t == NT - 1 and j + 1 < QT:
                            last.then_inc(acc_mm, 1)
                    last.then_inc(p_free, 1)

            def project_y(b, c):
                n = b * NCH + c
                pe.wait_ge(xl_ok, b * (2 * NCH) + NCH + c + 3)
                pe.wait_ge(y_ok, n)
                three(Y_BANK[:], w1T, slice(c * CH, (c + 1) * CH), slice(0, P)).then_inc(y_mm, 1)

            def project_first_y(b):
                pe.wait_ge(xh_ok, b * (2 * NCH) + NCH + 1)
                for i in range(H2):
                    for w in range(2):
                        mm(Y_BANK[:], w1T[:, w, i], xh[:, i, 0:CH], start=(i == 0 and w == 0), stop=False)
                pe.wait_ge(xl_ok, b * (2 * NCH) + NCH + 3)
                mm(Y_BANK[:], w1T[:, 0, 0], xl[:, 0, 0:CH], start=False, stop=False)
                mm(Y_BANK[:], w1T[:, 0, 1], xl[:, 1, 0:CH], start=False, stop=True).then_inc(y_mm, 1)

            def select(par, g):
                cols = slice(g * P, min((g + 1) * P, W2C))
                rows = P if g < 4 else 96
                mm(R_BANK[g][0:rows, :], selh[:, cols], yst[:, par], start=True, stop=True).then_inc(sel_mm, 1)

            moments(0, 0)
            pe.wait_ge(set_act, 3)
            pe.wait_ge(set_dve, mark["weights"])
            with pe.Fori(0, B) as b:
                for c in range(NCH):
                    def early(t, c=c):
                        if c and t < LEAD:
                            if t == 0:
                                pe.wait_ge(f_lo, b * NCH + c)
                                pe.wait_ge(g_lo, b * NCH + c)
                            if t == QT and c == 1:
                                pe.wait_ge(g_lo, b * NCH + 2)
                            i = (c - 1) * LEAD + t
                            piece(b * (NT * NCH) + i, t, c - 1, i % 2)

                    queries(b, c)
                    early(0)
                    keys(b, c)
                    early(1)
                    values(b, c, 0)
                    early(2)
                    if c < NCH - 1:
                        values(b, c, 1)
                    early(3)
                    if c < NCH - 1:
                        early(4)
                pe.wait_ge(f_lo, b * NCH + NCH)
                for i, (t, c) in enumerate(LAST_PIECES):
                    if i == 2:
                        values(b, NCH - 1, 1)
                    i += FIRST_LAST
                    piece(b * (NT * NCH) + i, t, c, i % 2)
                pe.wait_ge(t_free, b * (NT * NCH) + NCH * LEAD + 2)
                for t in range(QT):
                    pe.wait_ge(m_rows, b * NT + t + 1)
                    mm(tps[0][:, t * P:(t + 1) * P], mrow[:, t], idh[:], start=True, stop=True).then_inc(m_mm, 1)
                pe.wait_ge(m_ok, b * NT + 2 * QT)
                pe.wait_ge(g_lo, b * NCH + NCH)
                pe.wait_ge(h_lo, 2 * (b * NCH + NCH))
                for t in range(2):
                    scores(0, t, 0, t, first=True)
                group(b, 0, 0)
                with pe.Fori(0, NCH - 2) as J:
                    for q in (1, 2, 3):
                        group(b, J, q)
                    group(b, J + 1, 0, finish=True)
                for q in (1, 2):
                    group(b, NCH - 2, q)
                group(b, NCH - 2, 3, maxima=False)
                group(b, NCH - 1, 0, maxima=False, rows=False, finish=True)
                for q in (1, 2):
                    group(b, NCH - 1, q, maxima=False, rows=False)
                group(b, NCH - 1, 3, maxima=False, rows=False, end=True)
                for h in range(H2):
                    transposed(b * NCH + NCH - 1, h)
                moments(2 * b + 1, 1)
                pe.wait_ge(gn_dve, (b * 2 + 1) * GN_STEPS + 4)
                project_first_y(b)
                project_y(b, 1)
                pe.wait_ge(yl_ok, b * NCH + 1)
                for g in range(5):
                    select(0, g)
                for c in range(NCH):
                    n = b * NCH + c

                    def z(g, c=c, n=n):
                        pe.wait_ge(qh_ok, 5 * n + g + 1)
                        if g == 4:
                            pe.wait_ge(ql_ok, 5 * n + 5)
                            for h in range(H2):
                                mm(Z_BANK[h][:], w2r[:, h * P:(h + 1) * P], qh[4][0:96, :], start=False,
                                   stop=True).then_inc(z_mm, 1)
                            return
                        for h in range(H2):
                            for w in range(2):
                                mm(Z_BANK[h][:], w2T[:, w, g, h * P:(h + 1) * P], qh[g],
                                   start=(g == 0 and w == 0), stop=False)
                        pe.wait_ge(ql_ok, 5 * n + g + 1)
                        for h in range(H2):
                            mm(Z_BANK[h][:], w2T[:, 2, g, h * P:(h + 1) * P], ql[g], start=False, stop=False)

                    more = c + 1 < NCH
                    if c == NORM_AT + 1:
                        pe.wait_ge(gn_dve, (b * 2 + 2) * GN_STEPS + 4)
                    if more and c:
                        project_y(b, c + 1)
                    if c:
                        pe.wait_ge(z_ok, 2 * n)
                    z(0)
                    z(1)
                    z(2)
                    if more:
                        pe.wait_ge(yl_ok, n + 2)
                        for g in range(3):
                            select((c + 1) % 2, g)
                    z(3)
                    if more:
                        select((c + 1) % 2, 3)
                    if c == NORM_AT:
                        pe.wait_ge(y_ok, n + 2)
                        moments(2 * b + 2, 0)
                    z(4)
                    if more:
                        select((c + 1) % 2, 4)
                pe.wait_ge(z_ok, 2 * (b * NCH + NCH))


def kernel(x, L0_conv_Wq, L0_conv_bq, L0_conv_Wk, L0_conv_bk, L0_conv_Wv, L0_conv_bv, L0_conv_gamma,
           L1_conv_w1, L1_conv_b1, L1_conv_g1, L1_conv_be1, L1_conv_m1, L1_conv_v1,
           L1_conv_w2, L1_conv_b2, L1_conv_g2, L1_conv_be2, L1_conv_m2, L1_conv_v2):
    import concourse.bacc as bacc
    import numpy as np
    from concourse.bass_utils import run_bass_kernel_spmd

    f = np.float32
    base = [sum(MID - e for e in range(d)) for d in range(MID + 1)]

    def column(i, c):
        lo, hi = sorted((c, (c + i) % MID))
        return base[hi - lo] + lo

    order = [column(i, c) for i in range(MID // 2) for c in range(MID)]
    rest = [column(MID // 2, c) for c in range(REM)]
    w2p = np.zeros((C, W2C), f)
    w2p[:, :4 * P] = np.asarray(L1_conv_w2)[:, order]
    sel = np.zeros((2 * MID, W2C), np.float16)
    for i in range(MID // 2):
        for c in range(MID):
            sel[(c + i) % MID, i * MID + c] = 1
            sel[MID + (c + i) % MID, i * MID + c] = 1 / LO
    for r in range(3):
        at = 4 * P + r * 32
        w2p[:, at:at + REM] = np.asarray(L1_conv_w2)[:, rest]
        for c in range(REM):
            sel[(c + MID // 2) % MID, at + c] = 1
            sel[MID + (c + MID // 2) % MID, at + c] = 1 / LO

    vec = np.zeros((P, V_N), f)
    for k, v in ((V_BQ, L0_conv_bq), (V_BK, L0_conv_bk)):
        vec[:96, k] = np.tile(np.asarray(v), 3)
    vec[:, V_GAMMA] = np.asarray(L0_conv_gamma)[0]
    for k, v in ((V_B1, L1_conv_b1), (V_G1, L1_conv_g1), (V_BE1, L1_conv_be1), (V_M1, L1_conv_m1),
                 (V_V1, L1_conv_v1)):
        vec[:, k] = np.tile(np.asarray(v), 4)
    for k, v in ((V_BV, L0_conv_bv), (V_B2, L1_conv_b2), (V_G2, L1_conv_g2), (V_BE2, L1_conv_be2),
                 (V_M2, L1_conv_m2), (V_V2, L1_conv_v2)):
        vec[:, k:k + 2] = np.asarray(v).reshape(2, P).T
    vec[96:98, V_FROW] = M_ROWS
    arrays = {
        "x": np.ascontiguousarray(np.asarray(x).reshape(B, C, HW)),
        "wq": np.tile(np.asarray(L0_conv_Wq), (3, 1)),
        "wk": np.tile(np.asarray(L0_conv_Wk), (3, 1)),
        "wv": np.ascontiguousarray(np.asarray(L0_conv_Wv).reshape(H2, P, C).transpose(1, 0, 2)),
        "w1": np.tile(np.asarray(L1_conv_w1), (4, 1)),
        "w2": np.ascontiguousarray(w2p.reshape(H2, P, W2C).transpose(1, 0, 2)),
        "vec": vec,
        "ident": np.eye(P, dtype=f),
        "gmean": np.kron(np.eye(P // GROUP, dtype=f), np.full((GROUP, GROUP), 1 / GROUP, f)),
        "sel": sel,
    }
    nc = bacc.Bacc("TRN2", target_bir_lowering=False, num_devices=1)
    args = [nc.dram_tensor(k, a.shape, mybir.dt.from_np(a.dtype), kind="ExternalInput").ap()
            for k, a in arrays.items()]
    args.append(nc.dram_tensor("out", (B, C, HW), mybir.dt.float32, kind="ExternalOutput").ap())
    build(nc, *args)
    r = run_bass_kernel_spmd(nc, [arrays], core_ids=[0])
    return r.results[0]["out"].reshape(B, C, 64, 64)
```

```python
from contextlib import ExitStack

import concourse.bass as bass
from concourse import mybir

B, C, HW = 4, 256, 4096
CK = C // 8
MID = 32
PAIRS = MID * (MID + 1) // 2
P = 128
CH = 512
NCH = HW // CH
NT = HW // P
QT = CH // P
H2 = C // P
GROUP = 8
REM = PAIRS - 4 * P
W2C = 4 * P + 96
GN_EPS = 1e-5
BN_EPS = 1e-5
GN_MAX = 182.0
TINY = 1e-30
F16_TOP = 2.0 ** 15
QK_TOP = 2.0 ** 14
M_ROWS = (2.0 ** 14, 2.0 ** 3)
LO = 2.0 ** 11
EXP_SHIFT = 8.0
SLOTS = 4
LEAD = 5

V_BQ, V_BK, V_BV, V_GAMMA, V_B1, V_G1, V_BE1, V_M1, V_V1 = 0, 1, 2, 4, 5, 6, 7, 8, 9
V_B2, V_G2, V_BE2, V_M2, V_V2, V_FROW, V_N = 10, 12, 14, 16, 18, 20, 21


def build(nc, x, wq, wk, wv, w1, w2, vec, ident, gmean, sel, out):
    f32, f16 = mybir.dt.float32, mybir.dt.float16
    ACT = mybir.ActivationFunctionType
    ALU = mybir.AluOpType
    AX = mybir.AxisListType.X
    ds = bass.ds
    ctx = ExitStack()
    with ctx:
        def sb(name, shape, dt):
            return ctx.enter_context(nc.sbuf_tensor(name, shape, dt))

        def sem(name):
            return ctx.enter_context(nc.semaphore(name))

        xa = sb("xa", [P, H2, HW], f32)
        xs = sb("xs", [P, H2, HW], f32)
        xh = sb("xh", [P, H2, HW], f16)
        xl = sb("xl", [P, H2, HW], f16)
        fst = sb("fst", [P, HW], f16)
        gst = sb("gst", [P, HW], f16)
        xn = sb("xn", [P, 2, H2, CH], f32)
        hth = sb("hth", [P, NT, C + 1], f16)
        htl = sb("htl", [P, NT, C], f16)
        p32 = sb("p32", [P, SLOTS, CH], f32)
        ph = sb("ph", [P, SLOTS, CH], f16)
        pl = sb("pl", [P, SLOTS, CH], f16)
        mx = sb("mx", [P, NT, NCH], f32)
        nm = sb("nm", [P, QT], f32)
        mw = sb("mw", [P, 5, QT], f32)
        r1 = sb("r1", [P, QT], f32)
        r2 = sb("r2", [P, QT], f32)
        r3 = sb("r3", [P, QT], f32)
        mrow = sb("mrow", [P, QT, P], f16)
        rinv = sb("rinv", [P, QT], f32)
        ot = sb("ot", [P, QT, C], f32)
        bst = [sb(f"bst{i}", [P, H2, NCH, 6], f32) for i in range(2)]
        bag = [sb(f"bag{i}", [P, H2, 2], f32) for i in range(2)]
        gin = [sb(f"gin{i}", [P, H2, 2], f32) for i in range(2)]
        gsb = [sb(f"gsb{i}", [P, H2, 2], f32) for i in range(2)]
        gmq = [sb(f"gmq{i}", [P, H2], f32) for i in range(2)]
        gve = [sb(f"gve{i}", [P, H2], f32) for i in range(2)]
        rstd = [sb(f"rstd{i}", [P, H2], f32) for i in range(2)]
        nbias = [sb(f"nbias{i}", [P, H2], f32) for i in range(2)]
        ht32 = htl[:].rearrange("p t c -> p (t c)").bitcast(f32)
        ht16 = htl[:].rearrange("p t c -> p (t c)")
        pb = ht32[:, 0:5 * CH].rearrange("p (g n) -> p g n", g=5)
        ybig = ht32[:, 5 * CH:7 * CH].rearrange("p (r n) -> p r n", r=2)
        yst = ht16[0:64, 14 * CH:16 * CH].rearrange("p (r n) -> p r n", r=2)
        qrest = sb("qrest", [P, CH], f16)
        qh = [pl[:, g] for g in range(4)] + [qrest[:]]
        ql = [ph[:, g] for g in range(4)]
        zt = p32[:].rearrange("p (r h) n -> p r h n", r=2)
        og = sb("og", [P, 2, H2, CH], f32)
        wqn = sb("wqn", [96, C], f32)
        wkn = sb("wkn", [96, C], f32)
        wvn = zt[:, 0, :, 0:C]
        w1n = sb("w1n", [P, C], f32)
        w2n = og[:].rearrange("p a h n -> p (a h n)")[:, 0:H2 * W2C].rearrange("p (h n) -> p h n", h=H2)
        vs = sb("vs", [P, V_N], f32)
        idn = sb("idn", [P, P], f32)
        idh = sb("idh", [P, P], f16)
        gm = sb("gm", [P, P], f32)
        ones = sb("ones", [P, P], f32)
        selh = sb("selh", [64, W2C], f16)
        wqT = sb("wqT", [P, 2, H2, 96], f16)
        wkT = sb("wkT", [P, 2, H2, 96], f16)
        wvT = sb("wvT", [P, 2, H2, C], f16)
        w1T = sb("w1T", [P, 2, H2, P], f16)
        w2T = sb("w2T", [P, 3, 4, C], f16)
        w2r = sb("w2r", [96, C], f16)
        sc = sb("sc", [P, 64], f32)
        exps = sb("exps", [P, 4], f32)
        carrier = sb("carrier", [P, 1], f32)
        spare = sb("spare", [P, 16], f32)
        bq = sb("bq", [96, 1], f32)
        bk = sb("bk", [96, 1], f32)
        esc = sb("esc", [P, 1], f32)
        vout = sb("vout", [P, H2], f32)
        gbv = sb("gbv", [P, H2], f32)
        s1a = sb("s1a", [P, 1], f32)
        t1a = sb("t1a", [P, 1], f32)
        sc2 = sb("sc2", [P, H2], f32)
        t2 = sb("t2", [P, H2], f32)

        acc = [ctx.enter_context(nc.psum_tensor(f"acc{i}", [P, CH], f32)) for i in range(QT)]
        sps = [ctx.enter_context(nc.psum_tensor(f"sps{i}", [P, CH], f32)) for i in range(2)]
        tps = [ctx.enter_context(nc.psum_tensor(f"tps{i}", [P, CH], f32)) for i in range(2)]

        w_in = sem("w_in")
        x_in = [sem(f"x_in{c}") for c in range(NCH)]
        x_next = sem("x_next")
        st_ok = sem("st_ok")
        set_dve = sem("set_dve")
        set_pool = sem("set_pool")
        set_pe = sem("set_pe")
        set_act = sem("set_act")
        gn_dve = sem("gn_dve")
        gn_in = sem("gn_in")
        gn_pe = sem("gn_pe")
        gn_var = sem("gn_var")
        gn_pow = sem("gn_pow")
        gn_ok = sem("gn_ok")
        xh_ok = sem("xh_ok")
        xh_half = sem("xh_half")
        xn_act, xn_dve = sem("xn_act"), sem("xn_dve")
        xn_first = sem("xn_first")
        xl_ok = sem("xl_ok")
        f_mm, g_mm, h_mm = sem("f_mm"), sem("g_mm"), sem("h_mm")
        f_hi, g_hi, h_hi = sem("f_hi"), sem("g_hi"), sem("h_hi")
        f_lo, g_lo, h_lo = sem("f_lo"), sem("g_lo"), sem("h_lo")
        t_mm = sem("t_mm")
        t_free = sem("t_free")
        nm_ok = sem("nm_ok")
        m_pool = sem("m_pool")
        m_rows = sem("m_rows")
        m_mm = sem("m_mm")
        m_ok = sem("m_ok")
        s_mm = sem("s_mm")
        ph_ok, p32_ok, pl_ok = sem("ph_ok"), sem("p32_ok"), sem("pl_ok")
        p_free = sem("p_free")
        acc_mm = sem("acc_mm")
        rinv_ok = sem("rinv_ok")
        ot_act = sem("ot_act")
        ot_dve = sem("ot_dve")
        o_mm = sem("o_mm")
        x1_ok = sem("x1_ok")
        bv_ok = sem("bv_ok")
        y_mm, y_ok, yh_ok, yl_ok = sem("y_mm"), sem("y_ok"), sem("yh_ok"), sem("yl_ok")
        sel_mm = sem("sel_mm")
        pb_ok, qh_ok, ql_ok = sem("pb_ok"), sem("qh_ok"), sem("ql_ok")
        z_mm = sem("z_mm")
        z_ok = sem("z_ok")
        res_ok = sem("res_ok")
        og_free = [sem("og_free0"), sem("og_free1")]
        block = ctx.enter_context(nc.Block())

        class Steps:

            def __init__(self, eng, s, base=0):
                self.eng, self.s, self.base, self.n = eng, s, base, 0

            def __call__(self, ins):
                ins.then_inc(self.s, 1)
                self.n += 1
                self.eng.wait_ge(self.s, self.base + self.n)

        AHEAD = 3
        LAST_PIECES = [(t, NCH - 1) for t in range(QT)] + [(QT, NCH - 2), (QT, NCH - 1)]
        FIRST_LAST = (NCH - 1) * LEAD - 1
        FIRST = 4
        NORM_AT = NCH - 4
        SPLITS = NT - QT + 1
        NLOADS = 9
        GN_STEPS = 5
        M_STEPS = 4

        xv = x.rearrange("b (h p) n -> b p h n", p=P)
        ov = out.rearrange("b (h p) n -> b p h n", p=P)
        R_BANK = [acc[1], acc[2], acc[3], tps[0], tps[1]]
        Y_BANK = acc[0]
        Z_BANK = sps

        (K_NQ, K_NK, K_PR, K_C2, K_A, K_BB, K_T, K_RS1, K_INV1, K_T1, K_YB, K_A2, K_AA, K_IA) = range(14)
        K_RV, K_RW, K_INV2, K_MX, K_U, K_W = 16, 18, 20, 22, 24, 26
        mark = {}

        def h_bank(c, k):
            return acc[2 * (c % 2) + k]

        def fg_bank(c):
            return sps if c else acc[2:]

        @block.sync
        def _(sp):
            for dst, src in ((vs[:], vec), (wqn[:], wq), (wkn[:], wk), (wvn, wv), (w1n[:], w1), (w2n, w2), (idn[:], ident),
                             (gm[:], gmean), (selh[:], sel)):
                sp.dma_start(dst, src).then_inc(w_in, 16)
            for c in range(NCH):
                sp.dma_start(xa[:, :, c * CH:(c + 1) * CH], xv[0, :, :, c * CH:(c + 1) * CH]).then_inc(x_in[c], 16)

            def store(b, c):
                sp.wait_ge(res_ok, b * NCH + c + 1)
                sp.dma_start(ov[ds(b, 1), :, :, c * CH:(c + 1) * CH].rearrange("a p h n -> (a p) h n"),
                             og[:, c % 2]).then_inc(og_free[c % 2], 16)

            with sp.Fori(0, B - 1) as b:
                for c in range(NCH):
                    sp.wait_ge(x1_ok, 2 * (b * NCH + c + 1))
                    sp.dma_start(xa[:, :, c * CH:(c + 1) * CH],
                                 xv[ds(b + 1, 1), :, :, c * CH:(c + 1) * CH].rearrange("a p h n -> (a p) h n")
                                 ).then_inc(x_next, 16)
                    sp.wait_ge(x_next, 16 * (b * NCH + c + 1))
                for c in range(NCH):
                    store(b, c)
            sp.sem_inc(x_next, 16 * NCH)
            for c in range(NCH):
                store(B - 1, c)
            for par in range(2):
                sp.wait_ge(og_free[par], 16 * (B * NCH // 2 + 1))

        @block.vector
        def _(dve):
            V = nc.vector
            s = Steps(dve, set_dve)

            def col(k, n=1, p=P):
                return sc[0:p, k:k + n]

            def vc(k, n=1, p=P):
                return vs[0:p, k:k + n]

            carried = [0]

            def carry_wait():
                carried[0] = (carried[0] + 1) % 16
                V.memset(spare[:, carried[0]:carried[0] + 1], 0.0)

            counted = [0]

            def first_stats():
                c, h = divmod(counted[0], H2)
                counted[0] += 1
                if h == 0:
                    dve.wait_ge(x_in[c], 16)
                ins = V.bn_stats(bst[0][:, h, c], xa[:, h, c * CH:(c + 1) * CH])
                if counted[0] == H2 * NCH:
                    ins.then_inc(st_ok, 1)

            def over_stats(ins):
                ins.then_inc(set_dve, 1)
                s.n += 1
                if counted[0] < H2 * NCH:
                    first_stats()
                dve.wait_ge(set_dve, s.n)

            def magnitude(o, v, least, step=s):
                step(V.scalar_tensor_tensor(o, v, -1.0, v, ALU.mult, ALU.max))
                step(V.tensor_scalar(o, o, least, None, ALU.add))

            s(V.memset(gst[96:P, :], 0.0))
            mark["zeros"] = s.n
            dve.wait_ge(w_in, 16 * NLOADS)
            dve.wait_ge(set_pool, 1)
            s(V.tensor_scalar(col(K_W), vc(V_V1), BN_EPS, None, ALU.add))
            s(V.tensor_scalar(col(K_W + 1, 2), vc(V_V2, 2), BN_EPS, None, ALU.add))
            mark["variances"] = s.n
            s(V.tensor_copy(idh[:], idn[:]))
            s(V.tensor_reduce(col(K_NQ, 1, 96), wqn[:], AX, ALU.add, apply_absolute_value=True))
            s(V.tensor_reduce(col(K_NK, 1, 96), wkn[:], AX, ALU.add, apply_absolute_value=True))
            magnitude(col(K_U, 2, 96), vc(V_BQ, 2, 96), TINY)
            s(V.tensor_tensor(col(K_NQ, 2, 96), col(K_NQ, 2, 96), col(K_U, 2, 96), ALU.add))
            s(V.tensor_tensor(col(K_PR, 1, 96), col(K_NQ, 1, 96), col(K_NK, 1, 96), ALU.mult))
            mark["bounds"] = s.n
            dve.wait_ge(set_pe, 1)
            s(V.tensor_scalar(esc[:], tps[1][:, 0:1], GN_MAX ** 2 / QK_TOP ** 2, None, ALU.mult))
            over_stats(V.reciprocal(col(K_C2), esc[:]))
            over_stats(V.reciprocal(col(K_BB, 1, 96), col(K_NQ, 1, 96)))
            over_stats(V.scalar_tensor_tensor(col(K_T, 1, 96), col(K_NK, 1, 96), col(K_C2, 1, 96), col(K_BB, 1, 96),
                                     ALU.mult, ALU.mult))
            mark["ratio"] = s.n
            dve.wait_ge(set_pool, 3)
            over_stats(V.reciprocal(col(K_T, 1, 96), col(K_A, 1, 96)))
            over_stats(V.tensor_tensor(col(K_BB, 1, 96), col(K_T, 1, 96), col(K_C2, 1, 96), ALU.mult))
            over_stats(V.tensor_scalar(wqn[:], wqn[:], col(K_A, 1, 96), None, ALU.mult))
            over_stats(V.tensor_scalar(wkn[:], wkn[:], col(K_BB, 1, 96), None, ALU.mult))
            over_stats(V.tensor_tensor(bq[:], vc(V_BQ, 1, 96), col(K_A, 1, 96), ALU.mult))
            over_stats(V.tensor_tensor(bk[:], vc(V_BK, 1, 96), col(K_BB, 1, 96), ALU.mult))
            def moments(n, layer):
                g = Steps(dve, gn_dve, n * GN_STEPS)
                dve.wait_ge(st_ok, n + 1)
                carry_wait()
                for h in range(H2):
                    last = V.bn_aggr(bag[layer][:, h], bst[layer][:, h].rearrange("p c k -> p (c k)"))
                g(last)
                V.tensor_copy(gin[layer][:, :, 0], bag[layer][:, :, 0])
                g(V.tensor_tensor(gmq[layer][:], bag[layer][:, :, 0], bag[layer][:, :, 0], ALU.mult))
                V.tensor_tensor(gin[layer][:, :, 1], bag[layer][:, :, 1], gmq[layer][:], ALU.add).then_inc(gn_in, 1)

            over_stats(V.tensor_reduce(col(K_RV, 2), wvn, AX, ALU.add, apply_absolute_value=True))
            over_stats(V.tensor_scalar(col(K_RV, 2), col(K_RV, 2), TINY, GN_MAX / F16_TOP, ALU.add, ALU.mult))
            over_stats(V.reciprocal(col(K_RW, 2), col(K_RV, 2)))
            for h in range(H2):
                over_stats(V.tensor_scalar(wvn[:, h], wvn[:, h], col(K_RW + h), None, ALU.mult))
            over_stats(V.tensor_scalar(vout[:], col(K_RV, 2), vc(V_GAMMA), None, ALU.mult))
            over_stats(V.tensor_scalar(gbv[:], vc(V_BV, 2), vc(V_GAMMA), None, ALU.mult))
            over_stats(V.tensor_scalar(mw[:, 4], mw[:, 0], 0.0, col(K_C2), ALU.mult, ALU.add))
            over_stats(V.tensor_scalar(mw[:, 4], mw[:, 4], EXP_SHIFT, None, ALU.mult))
            mark["scaled_qkv"] = s.n
            over_stats(V.tensor_reduce(col(K_MX, 2), w2n, AX, ALU.max, apply_absolute_value=True))
            over_stats(V.tensor_scalar(col(K_MX, 2), col(K_MX, 2), TINY, 2.0 ** -14, ALU.add, ALU.mult))
            over_stats(V.reciprocal(col(K_U, 2), col(K_MX, 2)))
            for h in range(H2):
                over_stats(V.tensor_scalar(w2n[:, h], w2n[:, h], col(K_U + h), None, ALU.mult))
            over_stats(V.tensor_reduce(col(K_RS1), w1n[:], AX, ALU.add, apply_absolute_value=True))
            over_stats(V.tensor_tensor(col(K_INV1), vc(V_G1), col(K_W), ALU.mult))
            over_stats(V.tensor_tensor(col(K_YB), col(K_RS1), col(K_INV1), ALU.mult))
            over_stats(V.tensor_scalar(col(K_RS1), col(K_RS1), TINY, 2.0 ** -7, ALU.add, ALU.mult))
            over_stats(V.reciprocal(col(K_U), col(K_RS1)))
            over_stats(V.tensor_scalar(w1n[:], w1n[:], col(K_U), None, ALU.mult))
            mark["scaled"] = s.n
            over_stats(V.tensor_tensor(col(K_T1), vc(V_B1), vc(V_M1), ALU.subtract))
            over_stats(V.scalar_tensor_tensor(col(K_T1), col(K_T1), col(K_INV1), vc(V_BE1), ALU.mult, ALU.add))
            magnitude(col(K_T), col(K_YB), 0.0, over_stats)
            over_stats(V.tensor_scalar(col(K_YB), col(K_T), GN_MAX, None, ALU.mult))
            magnitude(col(K_U), col(K_T1), 1e-15, over_stats)
            over_stats(V.tensor_tensor(col(K_YB), col(K_YB), col(K_U), ALU.add))
            over_stats(V.tensor_tensor(col(K_YB), col(K_YB), col(K_YB), ALU.mult))
            mark["squares"] = s.n
            dve.wait_ge(set_act, 1)
            V.tensor_tensor(wqT[:, 1], acc[0][:, 0:192].rearrange("p (h c) -> p h c", h=2), wqT[:, 0], ALU.subtract)
            V.tensor_tensor(wkT[:, 1], acc[1][:, 0:192].rearrange("p (h c) -> p h c", h=2), wkT[:, 0], ALU.subtract)
            over_stats(V.tensor_tensor(wvT[:, 1], acc[2][:].rearrange("p (h c) -> p h c", h=2), wvT[:, 0], ALU.subtract))
            mark["weights_qkv"] = s.n
            while counted[0] < H2 * NCH:
                first_stats()
            moments(0, 0)
            dve.wait_ge(set_pe, 4)
            over_stats(V.tensor_scalar(col(K_T), tps[1][:, 8:9], 1.0 / F16_TOP, None, ALU.mult))
            over_stats(V.reciprocal(col(K_A2), col(K_T)))
            mark["square"] = s.n
            over_stats(V.tensor_tensor(col(K_INV2, 2), vc(V_G2, 2), col(K_W + 1, 2), ALU.mult))
            over_stats(V.tensor_tensor(t2[:], vc(V_B2, 2), vc(V_M2, 2), ALU.subtract))
            over_stats(V.tensor_tensor(t2[:], t2[:], col(K_INV2, 2), ALU.mult))
            over_stats(V.tensor_tensor(t2[:], t2[:], vc(V_BE2, 2), ALU.add))
            over_stats(V.tensor_tensor(col(K_INV2, 2), col(K_INV2, 2), col(K_MX, 2), ALU.mult))

            def variance(n, layer):
                g = Steps(dve, gn_dve, n * GN_STEPS + 2)
                gs, gq, gv = gsb[layer], gmq[layer], gve[layer]
                dve.wait_ge(gn_pe, n + 1)
                g(V.tensor_copy(gs[:].rearrange("p h k -> p (h k)"), Y_BANK[:, 0:4]))
                g(V.tensor_tensor(gq[:], gs[:, :, 0], gs[:, :, 0], ALU.mult))
                g(V.tensor_tensor(gv[:], gs[:, :, 1], gq[:], ALU.subtract))
                V.tensor_scalar(gv[:], gv[:], 0.0, GN_EPS, ALU.max, ALU.add).then_inc(gn_var, 1)

            def bias(n, layer):
                dve.wait_ge(gn_pow, n + 1)
                V.scalar_tensor_tensor(nbias[layer][:], gsb[layer][:, :, 0], -1.0, rstd[layer][:], ALU.mult,
                                       ALU.mult).then_inc(gn_ok, 1)

            def normed(b, c):
                at = slice(c * CH, (c + 1) * CH)
                dve.wait_ge(xl_ok, (b * 2 + 1) * NCH + c + 1)
                for h in range(H2 if c < AHEAD else 1):
                    last = V.tensor_scalar(xn[:, c % 2, h], xs[:, h, at], rstd[1][:, h:h + 1], nbias[1][:, h:h + 1],
                                           ALU.mult, ALU.add)
                last.then_inc(xn_dve, 1)

            def first_normed(b, c):
                dve.wait_ge(xl_ok, b * (2 * NCH) + c + 1)
                for h in range(H2):
                    last = V.tensor_scalar(xn[:, c % 2, h], xa[:, h, c * CH:(c + 1) * CH], rstd[0][:, h:h + 1],
                                           nbias[0][:, h:h + 1], ALU.mult, ALU.add)
                last.then_inc(xn_first, 1)

            def first_low(b, layer):
                for h in range(H2):
                    if h == 0:
                        dve.wait_ge(xh_half, b * 2 + layer + 1)
                    else:
                        dve.wait_ge(xh_ok, b * (2 * NCH) + layer * NCH + 1)
                    last = V.tensor_tensor(xl[:, h, 0:CH], xn[:, 0, h], xh[:, h, 0:CH], ALU.subtract)
                last.then_inc(xl_ok, 1)

            def query_low(n, c):
                at = slice(c * CH, (c + 1) * CH)
                dve.wait_ge(f_hi, n + 1)
                V.scalar_tensor_tensor(fst[64:96, at], fg_bank(c)[0][64:96, :], bq[64:96], fst[64:96, at],
                                       ALU.add, ALU.subtract).then_inc(f_lo, 1)

            def key_low(n, c):
                at = slice(c * CH, (c + 1) * CH)
                dve.wait_ge(g_hi, n + 1)
                V.scalar_tensor_tensor(gst[32:64, at], fg_bank(c)[1][32:64, :], bk[32:64], gst[32:64, at],
                                       ALU.add, ALU.subtract).then_inc(g_lo, 1)

            def value_low(n, c, k):
                dve.wait_ge(h_hi, 2 * n + k + 1)
                t = c * QT + 2 * k
                V.tensor_tensor(htl[:, t:t + 2], h_bank(c, k)[:].rearrange("p (t c) -> p t c", t=2),
                                hth[:, t:t + 2, 0:C], ALU.subtract).then_inc(h_lo, 1)

            def piece_max(n, tile, c, par):
                dve.wait_ge(t_mm, n + 1)
                V.reduce_max(mx[:, ds(tile, 1), c], tps[par][:], AX).then_inc(t_free, 1)

            def tile_max(n, tile, k):
                dve.wait_ge(t_free, n + 2)
                carry_wait()
                V.tensor_reduce(nm[:, k:k + 1], mx[:, ds(tile, 1)], AX, ALU.max, negate=True).then_inc(nm_ok, 1)

            def finish_block(n, J, half_):
                dve.wait_ge(o_mm, 2 * n + half_ + 1)
                at = ds(J * CH, CH)
                V.scalar_tensor_tensor(xs[:, half_, at], tps[half_][:], vout[:, half_:half_ + 1],
                                       xa[:, half_, at], ALU.mult, ALU.add).then_inc(x1_ok, 1)

            def stats(n, J, half_):
                dve.wait_ge(x1_ok, 2 * n + half_ + 1)
                return V.bn_stats(bst[1][:, half_, ds(J, 1)].rearrange("p a k -> p (a k)"), xs[:, half_, ds(J * CH, CH)])

            def next_stats(b, c, h):
                dve.wait_ge(x_next, 16 * (b * NCH + c + 1))
                return V.bn_stats(bst[0][:, h, ds(c, 1)].rearrange("p a k -> p (a k)"), xa[:, h, ds(c * CH, CH)])

            def divide(b, J):
                n = b * NCH + J
                for j in range(QT):
                    if j + 1 < QT:
                        dve.wait_ge(acc_mm, n * (QT - 1) + j + 1)
                    else:
                        dve.wait_ge(p_free, SLOTS + (n + 1) * NT)
                    V.reciprocal(rinv[:, j:j + 1], acc[j][:, C:C + 1]).then_inc(rinv_ok, 1)
                for j in (2, 3):
                    dve.wait_ge(rinv_ok, n * QT + j + 1)
                    V.tensor_scalar(ot[:, j], acc[j][:, 0:C], rinv[:, j:j + 1], None, ALU.mult).then_inc(ot_dve, 1)

            def group(b, J, q, maxima=True, pending=True, finish=False, closing=False):
                k = J * QT + q
                T = b * (NT * NCH) + J * NT + q * 8
                N = b * (NT * NCH) + (k + LEAD) * 8
                for u in range(8):
                    dve.wait_ge(p32_ok, T + u + 1)
                    V.tensor_tensor(pl[:, u % SLOTS], p32[:, u % SLOTS], ph[:, u % SLOTS],
                                    ALU.subtract).then_inc(pl_ok, 1)
                    if closing and u == 7:
                        if maxima:
                            piece_max(N + 6, k + LEAD, 6, 0)
                        divide(b, J)
                    if u == 0 and pending:
                        piece_max(N - 1, k + LEAD - 1, 7, 1)
                        tile_max(N, k + LEAD - 1, (q + LEAD - 1) % QT)
                    if finish and u in (2, 3):
                        if u == 2:
                            dve.wait_ge(bv_ok, b + 1)
                        finish_block(b * NCH + J - 1, J - 1, u - 2)
                    if finish and u in (3, 4):
                        stats(b * NCH + J - 1, J - 1, u - 3)
                    if finish and u in (6, 7):
                        next_stats(b, J - 1, u - 6)
                    if maxima and u and not (closing and u == 7):
                        piece_max(N + u - 1, k + LEAD, u - 1, (u - 1) % 2)

            def products(n, g, par):
                rows = P if g < 4 else 96
                dve.wait_ge(sel_mm, 5 * n + g + 1)
                dve.wait_ge(y_ok, n + 1)
                V.tensor_tensor(pb[0:rows, g], ybig[0:rows, par], R_BANK[g][0:rows, :],
                                ALU.mult).then_inc(pb_ok, 1)

            def product_low(n, g):
                dve.wait_ge(qh_ok, 5 * n + g + 1)
                if g < 4:
                    V.scalar_tensor_tensor(ql[g], qh[g], -LO, pb[:, g], ALU.mult,
                                           ALU.add).then_inc(ql_ok, 1)
                else:
                    V.scalar_tensor_tensor(qh[g][64:96, :], qh[g][64:96, :], -LO, pb[64:96, g], ALU.mult,
                                           ALU.add).then_inc(ql_ok, 1)

            def y_low(n, par):
                dve.wait_ge(yh_ok, n + 1)
                V.scalar_tensor_tensor(yst[32:64, par], yst[32:64, par], -LO, ybig[32:64, par], ALU.mult,
                                       ALU.add).then_inc(yl_ok, 1)

            variance(0, 0)
            dve.wait_ge(set_act, 2)
            V.tensor_tensor(w1T[:, 1], acc[3][:, 0:256].rearrange("p (h c) -> p h c", h=2), w1T[:, 0], ALU.subtract)
            V.tensor_tensor(w2T[:, 1, 0:2], sps[0][:].rearrange("p (g c) -> p g c", g=2), w2T[:, 0, 0:2], ALU.subtract)
            V.tensor_tensor(w2T[:, 1, 2:4], sps[1][:].rearrange("p (g c) -> p g c", g=2), w2T[:, 0, 2:4], ALU.subtract)
            s(V.tensor_tensor(w2r[32:64, :], tps[0][32:64, 0:C], w2r[32:64, :], ALU.subtract))
            mark["weights"] = s.n
            bias(0, 0)
            dve.wait_ge(gn_ok, 1)
            first_normed(0, 0)
            dve.wait_ge(xn_first, 1)
            first_low(0, 0)
            for c in range(1, AHEAD):
                first_normed(0, c)
            dve.wait_ge(set_pool, 4)
            s(V.tensor_tensor(col(K_T), col(K_AA), col(K_AA), ALU.mult))
            s(V.reciprocal(col(K_IA), col(K_T)))
            s(V.tensor_scalar(sc2[:], col(K_INV2, 2), col(K_IA), None, ALU.mult))
            s(V.tensor_scalar(col(K_AA), col(K_AA), LO, None, ALU.mult))
            s(V.tensor_tensor(col(K_T), col(K_INV1), col(K_RS1), ALU.mult))
            s(V.tensor_tensor(s1a[:], col(K_T), col(K_AA), ALU.mult))
            s(V.tensor_tensor(t1a[:], col(K_T1), col(K_AA), ALU.mult))
            with dve.Fori(0, B) as b:
                for c in range(NCH):
                    n = b * NCH + c

                    if AHEAD <= c + AHEAD < FIRST:
                        first_normed(b, c + AHEAD)

                    def early(t, c=c):
                        if c and t < LEAD:
                            i = (c - 1) * LEAD + t
                            piece_max(b * (NT * NCH) + i, t, c - 1, i % 2)

                    early(0)
                    query_low(n, c)
                    early(1)
                    key_low(n, c)
                    early(2)
                    if c < NCH - 1:
                        value_low(n, c, 0)
                    early(3)
                    if c < NCH - 1:
                        value_low(n, c, 1)
                    if c < NCH - 1:
                        early(4)
                for i, (t, c) in enumerate(LAST_PIECES):
                    i += FIRST_LAST
                    piece_max(b * (NT * NCH) + i, t, c, i % 2)
                    if (t, c) == (QT - 1, NCH - 1):
                        dve.wait_ge(t_free, b * (NT * NCH) + i + 1 + 2)
                        carry_wait()
                        V.tensor_reduce(nm[:, 0:QT], mx[:, 0:QT], AX, ALU.max, negate=True).then_inc(nm_ok, QT)
                for k in range(2):
                    value_low(b * NCH + NCH - 1, NCH - 1, k)
                for t in range(QT, LEAD):
                    dve.wait_ge(m_rows, b * NT + t - QT + 1)
                    tile_max(b * (NT * NCH) + NCH * LEAD, t, t % QT)
                group(b, 0, 0, pending=False)
                with dve.Fori(0, NCH - 2) as J:
                    for q in (1, 2, 3):
                        group(b, J, q, closing=(q == 3))
                    group(b, J + 1, 0, finish=True)
                for q in (1, 2, 3):
                    group(b, NCH - 2, q, maxima=(q < 3), closing=(q == 3))
                group(b, NCH - 1, 0, maxima=False, pending=False, finish=True)
                for q in (1, 2, 3):
                    group(b, NCH - 1, q, maxima=False, pending=False, closing=(q == 3))
                for h in range(H2):
                    finish_block(b * NCH + NCH - 1, NCH - 1, h)
                for h in range(H2):
                    last = stats(b * NCH + NCH - 1, NCH - 1, h)
                last.then_inc(st_ok, 1)
                moments(b * 2 + 1, 1)
                variance(b * 2 + 1, 1)
                bias(b * 2 + 1, 1)
                dve.wait_ge(gn_ok, b * 2 + 2)
                normed(b, 0)
                dve.wait_ge(xn_dve, b * NCH + 1)
                first_low(b, 1)
                for c in range(1, AHEAD):
                    normed(b, c)
                y_low(b * NCH, 0)
                products(b * NCH, 0, 0)
                products(b * NCH, 1, 0)
                for c in range(NCH):
                    n = b * NCH + c
                    more = c + 1 < NCH
                    product_low(n, 0)
                    products(n, 2, c % 2)
                    product_low(n, 1)
                    products(n, 3, c % 2)
                    if more:
                        y_low(n + 1, (c + 1) % 2)
                    product_low(n, 2)
                    products(n, 4, c % 2)
                    if c == NORM_AT + 1:
                        bias(b * 2 + 2, 0)
                        dve.wait_ge(gn_ok, b * 2 + 3)
                    product_low(n, 3)
                    if more:
                        products(n + 1, 0, (c + 1) % 2)
                    product_low(n, 4)
                    if more:
                        products(n + 1, 1, (c + 1) % 2)
                    if c + AHEAD < NCH:
                        normed(b, c + AHEAD)
                    if c > NORM_AT:
                        first_normed(b + 1, c - NORM_AT - 1)
                    if c == 0:
                        for h in range(H2):
                            last = next_stats(b, NCH - 1, h)
                        last.then_inc(st_ok, 1)
                    if c == 1:
                        moments(b * 2 + 2, 0)
                    if c == NORM_AT:
                        variance(b * 2 + 2, 0)

        @block.gpsimd
        def _(pool):
            nc.gpsimd.memset(exps[:, 0:3], -0.5).then_inc(xl_ok, 2)
            nc.gpsimd.memset(exps[:, 3:4], 0.5).then_inc(t_free, 2)
            nc.gpsimd.memset(carrier[:], 0.0).then_inc(z_ok, 2)
            nc.gpsimd.memset(mrow[:, 0:1], 0.0).then_inc(p_free, SLOTS)
            nc.gpsimd.memset(mrow[:, 1:2], 0.0).then_inc(ot_act, 2)
            nc.gpsimd.memset(ones[:, 0:P // 4], 1.0).then_inc(ot_dve, 2)
            nc.gpsimd.memset(mrow[:, 2:QT], 0.0).then_inc(m_ok, QT)
            nc.gpsimd.memset(hth[:, :, C:C + 1], 1.0).then_inc(og_free[0], 16)
            nc.gpsimd.memset(ones[:, P // 4:P // 2], 1.0).then_inc(og_free[1], 16)
            for i in range(2):
                nc.gpsimd.memset(mw[:, i], M_ROWS[i])
                nc.gpsimd.memset(mw[:, 2 + i], 1 / M_ROWS[i])
            nc.gpsimd.memset(ones[:, P // 2:], 1.0).then_inc(set_pool, 1)
            pool.wait_ge(set_pool, 1)
            pool.wait_ge(set_dve, mark["variances"])
            nc.gpsimd.tensor_tensor(sc[:, K_W:K_W + 3], sc[:, K_W:K_W + 3], exps[:, 0:3],
                                    ALU.pow).then_inc(set_pool, 1)
            pool.wait_ge(set_dve, mark["ratio"])
            nc.gpsimd.tensor_tensor(sc[0:96, K_A:K_A + 1], sc[0:96, K_T:K_T + 1], exps[0:96, 3:4],
                                    ALU.pow).then_inc(set_pool, 1)
            pool.wait_ge(set_dve, mark["square"])
            nc.gpsimd.tensor_tensor(sc[:, K_AA:K_AA + 1], sc[:, K_A2:K_A2 + 1], exps[:, 3:4],
                                    ALU.pow).then_inc(set_pool, 1)

            def power(n, layer):
                pool.wait_ge(gn_var, n)
                nc.gpsimd.tensor_tensor(rstd[layer][:], gve[layer][:], exps[:, 0:2], ALU.pow).then_inc(gn_pow, 1)

            def low(b, layer, c):
                at = slice(c * CH, (c + 1) * CH)
                pool.wait_ge(xh_ok, (b * 2 + layer) * NCH + c + 1)
                if layer:
                    pool.wait_ge(xn_dve, b * NCH + c + 1)
                elif c < FIRST:
                    pool.wait_ge(xn_first, b * FIRST + c + 1)
                else:
                    pool.wait_ge(xn_act, b * (NCH - FIRST) + c + 1 - FIRST)
                for h in range(H2):
                    last = nc.gpsimd.tensor_tensor(xl[:, h, at], xn[:, c % 2, h], xh[:, h, at], ALU.subtract)
                last.then_inc(xl_ok, 1)

            def split_max(n, k, splits):
                pool.wait_ge(nm_ok, n + 1)
                pool.wait_ge(m_ok, n + 1)
                wide = k.stop - k.start
                step = Steps(pool, m_pool, splits * M_STEPS)
                tt = nc.gpsimd.tensor_tensor

                def wt(i):
                    return mw[:, i, 0:wide]

                step(tt(r3[:, k], nm[:, k], wt(4), ALU.add))
                step(tt(mrow[:, k, 96], r3[:, k], wt(2), ALU.mult))
                step(tt(r2[:, k], mrow[:, k, 96], wt(0), ALU.mult))
                step(tt(r1[:, k], r3[:, k], r2[:, k], ALU.subtract))
                tt(mrow[:, k, 97], r1[:, k], wt(3), ALU.mult).then_inc(m_rows, wide)

            def residual(b, c):
                pool.wait_ge(z_ok, 2 * (b * NCH + c + 2))
                pool.wait_ge(og_free[c % 2], 16 * (b * (NCH // 2) + c // 2 + 1))
                for h in range(H2):
                    last = nc.gpsimd.tensor_tensor(og[:, c % 2, h], xs[:, h, c * CH:(c + 1) * CH],
                                                   zt[:, c % 2, h], ALU.add)
                last.then_inc(res_ok, 1)

            power(1, 0)
            pool.wait_ge(xl_ok, 3)
            for c in range(1, AHEAD):
                low(0, 0, c)
            with pool.Fori(0, B) as b:
                for c in range(AHEAD, NCH):
                    low(b, 0, c)
                pool.wait_ge(xh_ok, b * (2 * NCH) + NCH)
                pool.wait_ge(xn_act, b * (NCH - FIRST) + NCH - FIRST)
                pool.wait_ge(xn_first, b * FIRST + FIRST)
                nc.gpsimd.tensor_tensor(carrier[:], exps[:, 0:1], exps[:, 0:1], ALU.mult)
                for h in range(H2):
                    last = nc.gpsimd.tensor_scalar(xa[:, h], xa[:, h], 1.0, gbv[:, h:h + 1], ALU.mult, ALU.add)
                last.then_inc(bv_ok, 1)
                split_max(b * NT + QT - 1, slice(0, QT), b * SPLITS)
                with pool.Fori(1, NT // QT) as jj:
                    for u in range(QT):
                        split_max(b * NT + jj * QT + u, slice(u, u + 1), b * SPLITS + 1 - QT + jj * QT + u)
                power(b * 2 + 2, 1)
                pool.wait_ge(xl_ok, b * (2 * NCH) + NCH + 3)
                for c in range(1, AHEAD):
                    low(b, 1, c)
                for c in range(NCH):
                    if c + AHEAD < NCH:
                        low(b, 1, c + AHEAD)
                    if c == NORM_AT:
                        power(b * 2 + 3, 0)
                    if c == NORM_AT + 1:
                        low(b + 1, 0, 0)
                    if c == NORM_AT + 2:
                        low(b + 1, 0, 1)
                    residual(b, c)
                low(b + 1, 0, 2)

        @block.scalar
        def _(act):
            A = nc.scalar.activation
            act.wait_ge(set_pool, 1)
            act.wait_ge(set_dve, mark["zeros"])
            act.wait_ge(w_in, 16 * NLOADS)
            A(fst[96:P, :], gst[96:P, :], ACT.Identity, bias=vs[96:P, V_FROW:V_FROW + 1])
            act.wait_ge(set_pe, 2)
            A(wqT[:, 0], acc[0][:, 0:192].rearrange("p (h c) -> p h c", h=2), ACT.Copy)
            A(wkT[:, 0], acc[1][:, 0:192].rearrange("p (h c) -> p h c", h=2), ACT.Copy)
            A(wvT[:, 0], acc[2][:].rearrange("p (h c) -> p h c", h=2), ACT.Copy).then_inc(set_act, 1)
            act.wait_ge(set_pe, 3)
            A(w1T[:, 0], acc[3][:, 0:256].rearrange("p (h c) -> p h c", h=2), ACT.Copy)
            A(w2T[:, 0, 0:2], sps[0][:].rearrange("p (g c) -> p g c", g=2), ACT.Copy)
            A(w2T[:, 0, 2:4], sps[1][:].rearrange("p (g c) -> p g c", g=2), ACT.Copy)
            A(w2r[:], tps[0][0:96, 0:C], ACT.Copy).then_inc(set_act, 1)
            act.wait_ge(set_act, 2)
            A(w2T[:, 2], w2T[:, 0], ACT.Copy, scale=1.0 / LO)
            A(w2r[64:96, :], w2r[64:96, :], ACT.Copy, scale=1.0 / LO).then_inc(set_act, 1)

            def high(b, layer, c, h):
                last = A(xh[:, h, c * CH:(c + 1) * CH], (xs if layer else xa)[:, h, c * CH:(c + 1) * CH],
                         ACT.Identity, bias=nbias[layer][:, h:h + 1], scale=rstd[layer][:, h:h + 1])
                if h == H2 - 1:
                    last.then_inc(xh_ok, 1)
                elif c == 0:
                    last.then_inc(xh_half, 1)

            def normed(b, c, h):
                if h == 0:
                    act.wait_ge(xl_ok, b * (2 * NCH) + c + 1)
                last = A(xn[:, c % 2, h], xa[:, h, c * CH:(c + 1) * CH], ACT.Identity,
                         bias=nbias[0][:, h:h + 1], scale=rstd[0][:, h:h + 1])
                if h == H2 - 1:
                    last.then_inc(xn_act, 1)

            def project_high(b, c):
                n = b * NCH + c
                at = slice(c * CH, (c + 1) * CH)
                norms = c + AHEAD < NCH
                floats = FIRST <= c + AHEAD < NCH

                def value_high(k):
                    act.wait_ge(h_mm, 2 * n + k + 1)
                    t = c * QT + 2 * k
                    A(hth[:, t:t + 2, 0:C], h_bank(c, k)[:].rearrange("p (t c) -> p t c", t=2),
                      ACT.Copy).then_inc(h_hi, 1)

                if norms:
                    for h in range(H2):
                        high(b, 0, c + AHEAD, h)
                act.wait_ge(f_mm, n + 1)
                A(fst[0:96, at], fg_bank(c)[0][0:96, :], ACT.Identity, bias=bq[:]).then_inc(f_hi, 1)
                if floats:
                    normed(b, c + AHEAD, 0)
                act.wait_ge(g_mm, n + 1)
                A(gst[0:96, at], fg_bank(c)[1][0:96, :], ACT.Identity, bias=bk[:]).then_inc(g_hi, 1)
                if floats:
                    normed(b, c + AHEAD, 1)
                value_high(0)
                value_high(1)

            def divide(b, J):
                for j in (0, 1):
                    act.wait_ge(rinv_ok, (b * NCH + J) * QT + j + 1)
                    A(ot[:, j], acc[j][:, 0:C], ACT.Copy, scale=rinv[:, j:j + 1]).then_inc(ot_act, 1)

            def group(b, J, q, rows=True, finish=False):
                k = J * QT + q
                T = b * (NT * NCH) + J * NT + q * 8
                for u in range(8):
                    act.wait_ge(s_mm, T + u + 1)
                    act.wait_ge(p_free, T + u + 1)
                    A(ph[:, u % SLOTS], sps[u % 2][:], ACT.Exp, scale=esc[:]).then_inc(ph_ok, 1)
                    A(p32[:, u % SLOTS], sps[u % 2][:], ACT.Exp, scale=esc[:]).then_inc(p32_ok, 1)
                    if finish and u == 1:
                        divide(b, J - 1)
                    if rows and u == 5:
                        act.wait_ge(m_mm, b * NT + k + LEAD)
                        A(gst[96:98, ds((k + LEAD - 1) * P, P)], tps[0][96:98, 0:P], ACT.Copy).then_inc(m_ok, 1)

            def y_out(n, par):
                act.wait_ge(y_mm, n + 1)
                A(ybig[:, par], Y_BANK[:], ACT.Relu, bias=t1a[:], scale=s1a[:]).then_inc(y_ok, 1)

            def y_high(n, par):
                act.wait_ge(y_ok, n + 1)
                A(yst[:, par], ybig[0:64, par], ACT.Copy, scale=1.0 / LO).then_inc(yh_ok, 1)

            def z_out(n, c):
                for h in range(H2):
                    act.wait_ge(z_mm, 2 * n + h + 1)
                    if c >= 2:
                        act.wait_ge(res_ok, n - 1)
                    A(zt[:, c % 2, h], Z_BANK[h][:], ACT.Relu, bias=t2[:, h:h + 1],
                      scale=sc2[:, h:h + 1]).then_inc(z_ok, 1)

            def product_high(n, g):
                rows = P if g < 4 else 96
                act.wait_ge(pb_ok, 5 * n + g + 1)
                A(qh[g][0:rows, :], pb[0:rows, g], ACT.Copy, scale=1.0 / LO).then_inc(qh_ok, 1)

            act.wait_ge(gn_ok, 1)
            for c in range(AHEAD):
                for h in range(H2):
                    high(0, 0, c, h)
            with act.Fori(0, B) as b:
                for c in range(NCH):
                    project_high(b, c)
                act.wait_ge(m_mm, b * NT + QT)
                A(gst[96:98, 0:CH], tps[0][96:98, :], ACT.Copy).then_inc(m_ok, QT)
                group(b, 0, 0)
                with act.Fori(0, NCH - 2) as J:
                    for q in (1, 2, 3):
                        group(b, J, q)
                    group(b, J + 1, 0, finish=True)
                for q in (1, 2, 3):
                    group(b, NCH - 2, q)
                group(b, NCH - 1, 0, rows=False, finish=True)
                for q in (1, 2, 3):
                    group(b, NCH - 1, q, rows=False)
                divide(b, NCH - 1)
                act.wait_ge(gn_ok, 2 * b + 2)
                for c in range(AHEAD - 1):
                    for h in range(H2):
                        high(b, 1, c, h)
                y_out(b * NCH, 0)
                y_high(b * NCH, 0)
                for h in range(H2):
                    high(b, 1, AHEAD - 1, h)
                product_high(b * NCH, 0)
                for c in range(NCH):
                    n = b * NCH + c
                    more = c + 1 < NCH
                    if c:
                        z_out(n - 1, c - 1)
                    if more:
                        y_out(n + 1, (c + 1) % 2)
                    product_high(n, 1)
                    if more:
                        y_high(n + 1, (c + 1) % 2)
                    product_high(n, 2)
                    if c + AHEAD < NCH:
                        act.wait_ge(xl_ok, (b * 2 + 1) * NCH + c + AHEAD + 1)
                        A(xn[:, (c + AHEAD) % 2, 1], xs[:, 1, (c + AHEAD) * CH:(c + AHEAD + 1) * CH], ACT.Identity,
                          bias=nbias[1][:, 1:2], scale=rstd[1][:, 1:2])
                        high(b, 1, c + AHEAD, 0)
                    product_high(n, 3)
                    if c + AHEAD < NCH:
                        high(b, 1, c + AHEAD, 1)
                    if c == NORM_AT + 1:
                        act.wait_ge(gn_ok, 2 * b + 3)
                    ahead = c in (NORM_AT + 1, NORM_AT + 2)
                    if ahead:
                        high(b + 1, 0, c - NORM_AT - 1, 0)
                    product_high(n, 4)
                    if ahead:
                        high(b + 1, 0, c - NORM_AT - 1, 1)
                    if more:
                        product_high(n + 1, 0)
                z_out(b * NCH + NCH - 1, NCH - 1)
                for h in range(H2):
                    high(b + 1, 0, 2, h)

        @block.tensor
        def _(pe):
            mm = nc.tensor.matmul
            pe.wait_ge(w_in, 16 * NLOADS)
            pe.wait_ge(set_pool, 1)
            pe.wait_ge(set_dve, mark["bounds"])
            mm(tps[1][:, 0:1], ones[0:CK, :], sc[0:CK, K_PR:K_PR + 1], start=True, stop=True).then_inc(set_pe, 1)
            tr = nc.tensor.transpose
            pe.wait_ge(set_dve, mark["scaled_qkv"])
            for i in range(H2):
                at = slice(i * P, (i + 1) * P)
                tr(acc[0][:, i * 96:(i + 1) * 96], wqn[:, at], idn[0:96, 0:96])
                tr(acc[1][:, i * 96:(i + 1) * 96], wkn[:, at], idn[0:96, 0:96])
                for o in range(H2):
                    last = tr(acc[2][:, i * C + o * P:i * C + (o + 1) * P], wvn[:, o, at], idn[:])
            last.then_inc(set_pe, 1)
            pe.wait_ge(set_dve, mark["scaled"])
            for i in range(H2):
                at = slice(i * P, (i + 1) * P)
                tr(acc[3][:, at], w1n[:, at], idn[:])
                for g in range(4):
                    tr(sps[g // 2][:, (g % 2) * C + i * P:(g % 2) * C + (i + 1) * P],
                       w2n[:, i, g * P:(g + 1) * P], idn[:])
                last = tr(tps[0][0:96, i * P:(i + 1) * P], w2n[:, i, 4 * P:W2C], idn[:])
            last.then_inc(set_pe, 1)
            pe.wait_ge(set_dve, mark["squares"])
            mm(tps[1][:, 8:9], ones[0:MID, :], sc[0:MID, K_YB:K_YB + 1], start=True, stop=True).then_inc(set_pe, 1)
            pe.wait_ge(set_dve, mark["weights_qkv"])

            def three(out, wT, at, cols):
                for i in range(H2):
                    for w, v in ((0, xh), (0, xl), (1, xh)):
                        last = mm(out, wT[:, w, i, cols], v[:, i, at], start=(i == 0 and w == 0 and v is xh),
                                  stop=(i == H2 - 1 and w == 1))
                return last

            def moments(n, layer):
                pe.wait_ge(gn_in, n + 1)
                mm(Y_BANK[:, 0:4], gm[:], gin[layer][:].rearrange("p h k -> p (h k)"), start=True,
                   stop=True).then_inc(gn_pe, 1)

            def queries(b, c):
                n = b * NCH + c
                if c:
                    pe.wait_ge(f_lo, n)
                three(fg_bank(c)[0][0:96, :], wqT, slice(c * CH, (c + 1) * CH), slice(0, 96)).then_inc(f_mm, 1)

            def keys(b, c):
                n = b * NCH + c
                if c:
                    pe.wait_ge(g_lo, n)
                three(fg_bank(c)[1][0:96, :], wkT, slice(c * CH, (c + 1) * CH), slice(0, 96)).then_inc(g_mm, 1)

            def values(b, c, k):
                n = b * NCH + c
                if c >= 2:
                    pe.wait_ge(h_lo, 2 * (n - 2) + k + 1)
                for e in range(2):
                    t = (c * QT + 2 * k + e) * P
                    for i in range(H2):
                        for w, v in ((0, xh), (1, xh), (0, xl)):
                            last = mm(h_bank(c, k)[:, e * C:(e + 1) * C], v[:, i, t:t + P], wvT[:, w, i],
                                      start=(i == 0 and w == 0 and v is xh), stop=(i == H2 - 1 and v is xl))
                last.then_inc(h_mm, 1)

            def piece(n, tile, c, par):
                pe.wait_ge(t_free, n + 1)
                mm(tps[par][:], gst[0:96, ds(tile * P, P)], fst[0:96, c * CH:(c + 1) * CH], start=True,
                   stop=True).then_inc(t_mm, 1)

            def scores(T, tile, J, par, first=False):
                if not first:
                    pe.wait_ge(p32_ok, T - 1)
                mm(sps[par][:], fst[:, tile * P:(tile + 1) * P], gst[:, ds(J * CH, CH)], start=True,
                   stop=True).then_inc(s_mm, 1)

            def transposed(n, h):
                pe.wait_ge(ot_act, 2 * (n + 2))
                pe.wait_ge(ot_dve, 2 * (n + 2))
                for j in range(QT):
                    last = tr(tps[h][:, j * P:(j + 1) * P], ot[:, j, h * P:(h + 1) * P], idn[:])
                last.then_inc(o_mm, 1)

            def group(b, J, q, maxima=True, rows=True, finish=False, end=False):
                k = J * QT + q
                T = b * (NT * NCH) + J * NT + q * 8
                N = b * (NT * NCH) + (k + LEAD) * 8
                for u in range(8):
                    t = q * 8 + u
                    if t + 2 < NT:
                        scores(T + u + 2, t + 2, J, u % 2)
                    elif not end:
                        if t + 2 == NT:
                            pe.wait_ge(m_ok, b * NT + (J + 2) * QT + QT)
                        scores(T + u + 2, t + 2 - NT, J + 1, u % 2)
                    if rows and u == 4:
                        tile = k + LEAD - 1
                        if maxima:
                            pe.wait_ge(t_free, N + u + 1)
                        pe.wait_ge(m_rows, b * NT + tile + 1)
                        mm(tps[0][:, 0:P], mrow[:, (q + LEAD - 1) % QT], idh[:], start=True,
                           stop=True).then_inc(m_mm, 1)
                    if finish and u in (2, 3):
                        n = b * NCH + J - 1
                        if maxima:
                            pe.wait_ge(t_free, N + u + 1)
                        transposed(n, u - 2)
                    if maxima and t == 0:
                        piece(N + u, k + LEAD, u, u % 2)
                    slot = u % SLOTS
                    pe.wait_ge(ph_ok, T + u + 1)
                    for j in range(QT):
                        if t == 0:
                            pe.wait_ge(ot_act if j < 2 else ot_dve, (b * NCH + J) * 2 + j % 2 + 1)
                        w = ph[:, slot, j * P:(j + 1) * P]
                        mm(acc[j][:, 0:C + 1], w, hth[:, t], start=(t == 0), stop=False)
                        mm(acc[j][:, 0:C], w, htl[:, t], start=False, stop=False)
                    if rows and u == 4:
                        pe.wait_ge(m_ok, b * NT + tile + 1 + QT)
                    if finish and u in (2, 3):
                        pe.wait_ge(x1_ok, 2 * n + u - 1)
                    if maxima and t:
                        piece(N + u, k + LEAD, u, u % 2)
                    pe.wait_ge(pl_ok, T + u + 1)
                    for j in range(QT):
                        last = mm(acc[j][:, 0:C + 1], pl[:, slot, j * P:(j + 1) * P], hth[:, t], start=False,
                                  stop=(t == NT - 1))
                        if t == NT - 1 and j + 1 < QT:
                            last.then_inc(acc_mm, 1)
                    last.then_inc(p_free, 1)

            def project_y(b, c):
                n = b * NCH + c
                pe.wait_ge(xl_ok, b * (2 * NCH) + NCH + c + 3)
                pe.wait_ge(y_ok, n)
                three(Y_BANK[:], w1T, slice(c * CH, (c + 1) * CH), slice(0, P)).then_inc(y_mm, 1)

            def project_first_y(b):
                for i in range(H2):
                    if i == 0:
                        pe.wait_ge(xh_half, b * 2 + 2)
                    else:
                        pe.wait_ge(xh_ok, b * (2 * NCH) + NCH + 1)
                    for w in range(2):
                        mm(Y_BANK[:], w1T[:, w, i], xh[:, i, 0:CH], start=(i == 0 and w == 0), stop=False)
                pe.wait_ge(xl_ok, b * (2 * NCH) + NCH + 3)
                mm(Y_BANK[:], w1T[:, 0, 0], xl[:, 0, 0:CH], start=False, stop=False)
                mm(Y_BANK[:], w1T[:, 0, 1], xl[:, 1, 0:CH], start=False, stop=True).then_inc(y_mm, 1)

            def select(par, g):
                cols = slice(g * P, min((g + 1) * P, W2C))
                rows = P if g < 4 else 96
                mm(R_BANK[g][0:rows, :], selh[:, cols], yst[:, par], start=True, stop=True).then_inc(sel_mm, 1)

            moments(0, 0)
            pe.wait_ge(set_act, 3)
            pe.wait_ge(set_dve, mark["weights"])
            with pe.Fori(0, B) as b:
                for c in range(NCH):
                    def early(t, c=c):
                        if c and t < LEAD:
                            if t == 0:
                                pe.wait_ge(f_lo, b * NCH + c)
                                pe.wait_ge(g_lo, b * NCH + c)
                            if t == QT and c == 1:
                                pe.wait_ge(g_lo, b * NCH + 2)
                            i = (c - 1) * LEAD + t
                            piece(b * (NT * NCH) + i, t, c - 1, i % 2)

                    pe.wait_ge(xl_ok, b * (2 * NCH) + c + 3)
                    if c == 1:
                        pe.wait_ge(z_ok, b * (2 * NCH) + 2)
                    queries(b, c)
                    early(0)
                    keys(b, c)
                    early(1)
                    values(b, c, 0)
                    early(2)
                    if c < NCH - 1:
                        values(b, c, 1)
                    early(3)
                    if c < NCH - 1:
                        early(4)
                pe.wait_ge(f_lo, b * NCH + NCH)
                for i, (t, c) in enumerate(LAST_PIECES):
                    i += FIRST_LAST
                    piece(b * (NT * NCH) + i, t, c, i % 2)
                values(b, NCH - 1, 1)
                pe.wait_ge(t_free, b * (NT * NCH) + NCH * LEAD + 2)
                for t in range(QT):
                    pe.wait_ge(m_rows, b * NT + t + 1)
                    mm(tps[0][:, t * P:(t + 1) * P], mrow[:, t], idh[:], start=True, stop=True).then_inc(m_mm, 1)
                pe.wait_ge(m_ok, b * NT + 2 * QT)
                pe.wait_ge(g_lo, b * NCH + NCH)
                for t in range(2):
                    scores(0, t, 0, t, first=True)
                pe.wait_ge(h_lo, 2 * (b * NCH + NCH))
                group(b, 0, 0)
                with pe.Fori(0, NCH - 2) as J:
                    for q in (1, 2, 3):
                        group(b, J, q)
                    group(b, J + 1, 0, finish=True)
                for q in (1, 2):
                    group(b, NCH - 2, q)
                group(b, NCH - 2, 3, maxima=False)
                group(b, NCH - 1, 0, maxima=False, rows=False, finish=True)
                for q in (1, 2):
                    group(b, NCH - 1, q, maxima=False, rows=False)
                group(b, NCH - 1, 3, maxima=False, rows=False, end=True)
                for h in range(H2):
                    transposed(b * NCH + NCH - 1, h)
                moments(2 * b + 1, 1)
                pe.wait_ge(gn_dve, (b * 2 + 1) * GN_STEPS + 3)
                project_first_y(b)
                project_y(b, 1)
                pe.wait_ge(yl_ok, b * NCH + 1)
                for g in range(5):
                    select(0, g)
                for c in range(NCH):
                    n = b * NCH + c

                    def z(g, c=c, n=n):
                        pe.wait_ge(qh_ok, 5 * n + g + 1)
                        if g == 4:
                            pe.wait_ge(ql_ok, 5 * n + 5)
                            for h in range(H2):
                                mm(Z_BANK[h][:], w2r[:, h * P:(h + 1) * P], qh[4][0:96, :], start=False,
                                   stop=True).then_inc(z_mm, 1)
                            return
                        for h in range(H2):
                            if g == 0 and c:
                                pe.wait_ge(z_ok, 2 * n + h + 1)
                            for w in range(2):
                                mm(Z_BANK[h][:], w2T[:, w, g, h * P:(h + 1) * P], qh[g],
                                   start=(g == 0 and w == 0), stop=False)
                        pe.wait_ge(ql_ok, 5 * n + g + 1)
                        for h in range(H2):
                            mm(Z_BANK[h][:], w2T[:, 2, g, h * P:(h + 1) * P], ql[g], start=False, stop=False)

                    more = c + 1 < NCH
                    if c == NORM_AT + 1:
                        pe.wait_ge(gn_dve, (b * 2 + 2) * GN_STEPS + 3)
                    if more and c:
                        project_y(b, c + 1)
                    z(0)
                    z(1)
                    z(2)
                    if more:
                        pe.wait_ge(yl_ok, n + 2)
                        for g in range(3):
                            select((c + 1) % 2, g)
                    z(3)
                    if more:
                        select((c + 1) % 2, 3)
                    if c == NORM_AT:
                        pe.wait_ge(y_ok, n + 2)
                        moments(2 * b + 2, 0)
                    z(4)
                    if more:
                        select((c + 1) % 2, 4)


def kernel(x, L0_conv_Wq, L0_conv_bq, L0_conv_Wk, L0_conv_bk, L0_conv_Wv, L0_conv_bv, L0_conv_gamma,
           L1_conv_w1, L1_conv_b1, L1_conv_g1, L1_conv_be1, L1_conv_m1, L1_conv_v1,
           L1_conv_w2, L1_conv_b2, L1_conv_g2, L1_conv_be2, L1_conv_m2, L1_conv_v2):
    import concourse.bacc as bacc
    import numpy as np
    from concourse.bass_utils import run_bass_kernel_spmd

    f = np.float32
    base = [sum(MID - e for e in range(d)) for d in range(MID + 1)]

    def column(i, c):
        lo, hi = sorted((c, (c + i) % MID))
        return base[hi - lo] + lo

    order = [column(i, c) for i in range(MID // 2) for c in range(MID)]
    rest = [column(MID // 2, c) for c in range(REM)]
    w2p = np.zeros((C, W2C), f)
    w2p[:, :4 * P] = np.asarray(L1_conv_w2)[:, order]
    sel = np.zeros((2 * MID, W2C), np.float16)
    for i in range(MID // 2):
        for c in range(MID):
            sel[(c + i) % MID, i * MID + c] = 1
            sel[MID + (c + i) % MID, i * MID + c] = 1 / LO
    for r in range(3):
        at = 4 * P + r * 32
        w2p[:, at:at + REM] = np.asarray(L1_conv_w2)[:, rest]
        for c in range(REM):
            sel[(c + MID // 2) % MID, at + c] = 1
            sel[MID + (c + MID // 2) % MID, at + c] = 1 / LO

    vec = np.zeros((P, V_N), f)
    for k, v in ((V_BQ, L0_conv_bq), (V_BK, L0_conv_bk)):
        vec[:96, k] = np.tile(np.asarray(v), 3)
    vec[:, V_GAMMA] = np.asarray(L0_conv_gamma)[0]
    for k, v in ((V_B1, L1_conv_b1), (V_G1, L1_conv_g1), (V_BE1, L1_conv_be1), (V_M1, L1_conv_m1),
                 (V_V1, L1_conv_v1)):
        vec[:, k] = np.tile(np.asarray(v), 4)
    for k, v in ((V_BV, L0_conv_bv), (V_B2, L1_conv_b2), (V_G2, L1_conv_g2), (V_BE2, L1_conv_be2),
                 (V_M2, L1_conv_m2), (V_V2, L1_conv_v2)):
        vec[:, k:k + 2] = np.asarray(v).reshape(2, P).T
    vec[96:98, V_FROW] = M_ROWS
    arrays = {
        "x": np.ascontiguousarray(np.asarray(x).reshape(B, C, HW)),
        "wq": np.tile(np.asarray(L0_conv_Wq), (3, 1)),
        "wk": np.tile(np.asarray(L0_conv_Wk), (3, 1)),
        "wv": np.ascontiguousarray(np.asarray(L0_conv_Wv).reshape(H2, P, C).transpose(1, 0, 2)),
        "w1": np.tile(np.asarray(L1_conv_w1), (4, 1)),
        "w2": np.ascontiguousarray(w2p.reshape(H2, P, W2C).transpose(1, 0, 2)),
        "vec": vec,
        "ident": np.eye(P, dtype=f),
        "gmean": np.kron(np.eye(P // GROUP, dtype=f), np.full((GROUP, GROUP), 1 / GROUP, f)),
        "sel": sel,
    }
    nc = bacc.Bacc("TRN2", target_bir_lowering=False, num_devices=1)
    args = [nc.dram_tensor(k, a.shape, mybir.dt.from_np(a.dtype), kind="ExternalInput").ap()
            for k, a in arrays.items()]
    args.append(nc.dram_tensor("out", (B, C, HW), mybir.dt.float32, kind="ExternalOutput").ap())
    build(nc, *args)
    r = run_bass_kernel_spmd(nc, [arrays], core_ids=[0])
    return r.results[0]["out"].reshape(B, C, 64, 64)
```
